# Optimizing a Trainium2 kernel written in Bass

```python
import numpy as np
import jax
import jax.numpy as jnp

def _softmax(x, axis=-1):
    return jax.nn.softmax(x, axis=axis)

def _gelu(x):
    return jax.nn.gelu(x, approximate=True)

def _silu(x):
    return jax.nn.silu(x)

def _sigmoid(x):
    return jax.nn.sigmoid(x)

def _layernorm(x, axis=-1, eps=1e-05):
    m = jnp.mean(x, axis=axis, keepdims=True)
    v = jnp.var(x, axis=axis, keepdims=True)
    return (x - m) / jnp.sqrt(v + eps)

def _scatter_add(tgt, idx, src, axis=0):
    return tgt.at[idx].add(src)

def _segment_sum(src, seg, n):
    return jax.ops.segment_sum(src, seg, n)
kernel_name = 'mk_prb_d1_jaxref_r4_4bfa24'

def setup_inputs(seed: int=0):
    np.random.seed(seed)
    _w = jnp.asarray

    def _L0_attn_setup():
        import jax, jax.numpy as jnp
        import numpy as np
        D_MODEL = 256
        EXP = 2
        D_IN = D_MODEL * EXP
        D_STATE = 16
        CONV_D = 4
        BATCH = 4
        SEQ = 512

        def _rmsnorm(x, w, eps=1e-06):
            return x * jax.lax.rsqrt(jnp.mean(x * x, axis=-1, keepdims=True) + eps) * w
        key = jax.random.key(seed)
        ks = jax.random.split(key, 8)
        sd = 1.0 / np.sqrt(D_MODEL)
        sdi = 1.0 / np.sqrt(D_IN)
        return {'x': jax.random.normal(ks[0], (BATCH, SEQ, D_MODEL), jnp.float32), 'norm_w': jnp.ones((D_MODEL,), jnp.float32), 'Win': jax.random.normal(ks[1], (D_MODEL, D_IN), jnp.float32) * sd, 'b_in': jnp.zeros((D_IN,), jnp.float32), 'conv_w': jax.random.normal(ks[2], (D_IN, 1, CONV_D), jnp.float32) * 0.5, 'conv_b': jnp.zeros((D_IN,), jnp.float32), 'A': jax.random.normal(ks[3], (D_IN, D_STATE, D_STATE), jnp.float32) * 0.1, 'Bm': jax.random.normal(ks[4], (D_IN, D_STATE, 1), jnp.float32), 'Cm': jax.random.normal(ks[5], (D_IN, 1, D_STATE), jnp.float32), 'Wout': jax.random.normal(ks[6], (D_IN, D_MODEL), jnp.float32) * sdi, 'b_out': jnp.zeros((D_MODEL,), jnp.float32)}
    _L0_attn_in = _L0_attn_setup()

    def _L0_ffn_setup():
        import jax, jax.numpy as jnp
        import numpy as np
        TOP_K = 2
        key = jax.random.key(seed)
        ks = jax.random.split(key, 8)
        B, S, D = (2, 512, 256)
        N_r, N_s = (16, 2)
        u = jax.random.normal(ks[0], (B, S, D), dtype=jnp.float32)
        centroids = jax.random.normal(ks[1], (N_r, D), dtype=jnp.float32)
        expert_biases = jnp.zeros((N_r,), dtype=jnp.float32)
        Wr = jax.random.normal(ks[2], (N_r, D, D), dtype=jnp.float32) * (1.0 / np.sqrt(D))
        br = jax.random.normal(ks[3], (N_r, D), dtype=jnp.float32) * 0.01
        Ws = jax.random.normal(ks[4], (N_s, D, D), dtype=jnp.float32) * (1.0 / np.sqrt(D))
        bs = jax.random.normal(ks[5], (N_s, D), dtype=jnp.float32) * 0.01
        return {'u': u, 'centroids': centroids, 'expert_biases': expert_biases, 'Wr': Wr, 'br': br, 'Ws': Ws, 'bs': bs}
    _L0_ffn_in = _L0_ffn_setup()
    _d = {'L0_attn_x': _L0_attn_in['x'], 'L0_attn_norm_w': _L0_attn_in['norm_w'], 'L0_attn_Win': _L0_attn_in['Win'], 'L0_attn_b_in': _L0_attn_in['b_in'], 'L0_attn_conv_w': _L0_attn_in['conv_w'], 'L0_attn_conv_b': _L0_attn_in['conv_b'], 'L0_attn_A': _L0_attn_in['A'], 'L0_attn_Bm': _L0_attn_in['Bm'], 'L0_attn_Cm': _L0_attn_in['Cm'], 'L0_attn_Wout': _L0_attn_in['Wout'], 'L0_attn_b_out': _L0_attn_in['b_out'], 'L0_ffn_centroids': _L0_ffn_in['centroids'], 'L0_ffn_expert_biases': _L0_ffn_in['expert_biases'], 'L0_ffn_Wr': _L0_ffn_in['Wr'], 'L0_ffn_br': _L0_ffn_in['br'], 'L0_ffn_Ws': _L0_ffn_in['Ws'], 'L0_ffn_bs': _L0_ffn_in['bs']}
    _x0 = _d['L0_attn_x']
    _d['L0_attn_x'] = jax.random.normal(jax.random.fold_in(jax.random.key(seed), 1), (8, 1024, 256), dtype=_x0.dtype)
    del _x0
    return _d

def reference(L0_attn_x, L0_attn_norm_w, L0_attn_Win, L0_attn_b_in, L0_attn_conv_w, L0_attn_conv_b, L0_attn_A, L0_attn_Bm, L0_attn_Cm, L0_attn_Wout, L0_attn_b_out, L0_ffn_centroids, L0_ffn_expert_biases, L0_ffn_Wr, L0_ffn_br, L0_ffn_Ws, L0_ffn_bs):

    def _L0_attn_ref(x, norm_w, Win, b_in, conv_w, conv_b, A, Bm, Cm, Wout, b_out):
        import jax, jax.numpy as jnp
        import numpy as np
        D_MODEL = 256
        EXP = 2
        D_IN = D_MODEL * EXP
        D_STATE = 16
        CONV_D = 4
        BATCH = 4
        SEQ = 512

        def _rmsnorm(x, w, eps=1e-06):
            return x * jax.lax.rsqrt(jnp.mean(x * x, axis=-1, keepdims=True) + eps) * w
        res = x
        h = _rmsnorm(x, norm_w)
        u = h @ Win + b_in
        u = u.transpose(0, 2, 1)
        u = jax.lax.conv_general_dilated(u, conv_w, window_strides=(1,), padding=[(CONV_D - 1, 0)], feature_group_count=D_IN, dimension_numbers=('NCH', 'OIH', 'NCH')) + conv_b[None, :, None]
        u = u.transpose(0, 2, 1)
        Bv = Bm[:, :, 0]
        Cv = Cm[:, 0, :]

        def step(hc, u_t):
            hc = jnp.einsum('bdr,drs->bds', hc, A) + u_t[:, :, None] * Bv[None]
            y = jnp.einsum('bds,ds->bd', hc, Cv)
            return (hc, y)
        h0 = jnp.zeros((x.shape[0], D_IN, D_STATE), u.dtype)
        _, ys = jax.lax.scan(step, h0, u.transpose(1, 0, 2))
        y = ys.transpose(1, 0, 2)
        return y @ Wout + b_out + res

    def _L0_ffn_ref(u, centroids, expert_biases, Wr, br, Ws, bs):
        import jax, jax.numpy as jnp
        import numpy as np
        TOP_K = 2
        N_r = centroids.shape[0]
        N_s = Ws.shape[0]
        raw_scores = jnp.einsum('bsd,ed->bse', u, centroids)
        s = jax.nn.softmax(raw_scores + expert_biases, axis=-1)
        topk_vals, topk_idx = jax.lax.top_k(s, TOP_K)
        g_topk = jnp.sum(jax.nn.one_hot(topk_idx, N_r, dtype=s.dtype) * topk_vals[..., None], axis=-2)
        xe = jnp.einsum('bsd,eod->bseo', u, Wr) + br
        routed = jnp.einsum('bse,bseo->bso', g_topk, xe)
        shared = (jnp.einsum('bsd,eod->bso', u, Ws) + jnp.sum(bs, axis=0)) / N_s
        return u + routed + shared
    x = L0_attn_x
    xn = _layernorm(x, axis=-1)
    x = x + _L0_attn_ref(xn, L0_attn_norm_w, L0_attn_Win, L0_attn_b_in, L0_attn_conv_w, L0_attn_conv_b, L0_attn_A, L0_attn_Bm, L0_attn_Cm, L0_attn_Wout, L0_attn_b_out) + _L0_ffn_ref(xn, L0_ffn_centroids, L0_ffn_expert_biases, L0_ffn_Wr, L0_ffn_br, L0_ffn_Ws, L0_ffn_bs)
    return x

_drawn_inputs = setup_inputs


def setup_inputs(seed=0):
    import zlib

    import numpy as np

    out = dict(_drawn_inputs(seed))
    spreads = {'L0_attn_norm_w': (1.0, 0.2),
     'L0_attn_b_in': (0.0, 0.1),
     'L0_attn_conv_b': (0.0, 0.1),
     'L0_attn_b_out': (0.0, 0.474),
     'L0_ffn_expert_biases': (0.0, 2.0)}
    factors = {'L0_ffn_br': 33.845, 'L0_ffn_bs': 47.955}
    for name, (base, spread) in spreads.items():
        noise = np.random.default_rng([zlib.crc32(name.encode()), seed]).standard_normal(out[name].shape)
        drawn = base * np.exp(spread * noise) if base else spread * noise
        out[name] = jnp.asarray(drawn.astype(out[name].dtype))
    for name, factor in factors.items():
        out[name] = (out[name] * factor).astype(out[name].dtype)
    return out
```

```python
import numpy as np
import concourse.bass as bass
from concourse import mybir
from contextlib import ExitStack

F32 = mybir.dt.float32
U32 = mybir.dt.uint32
ALU = mybir.AluOpType
ACT = mybir.ActivationFunctionType
AX = mybir.AxisListType

P = 128
BATCH, SEQ, D = 8, 1024, 256
DIN, NST, TAPS = 512, 16, 4
NE, NSH, TOPK = 16, 2, 2
NTOK = BATCH * SEQ
NT = NTOK // P
NCH = SEQ // P
KD = D // P
KI = DIN // P
CG = P // NST
NG = DIN // CG
GB = 4
NB = NG // GB
CB = CG * GB
HALO = TAPS - 1
PAIRS = NE // 2
LEVELS = 7
TROWS = 2 * P - 1


def wait_apart(eng, sem, value, passed):
    eng.wait_ge(sem, value)
    eng.sem_inc(passed, 1)


def phase1(nc, t, U, partial):
    ctx = ExitStack()
    with ctx:
        def sb(name, shape, dt=F32):
            return ctx.enter_context(nc.sbuf_tensor(name, shape, dt))

        def pb(name, shape, dt=F32):
            return ctx.enter_context(nc.psum_tensor(name, shape, dt))

        def sem(name):
            return ctx.enter_context(nc.semaphore(name))

        W = sb("W", [P, KD, NE * D])
        WS = sb("WS", [P, KD, D])
        WSraw = sb("WSraw", [P, KD, NSH, D])
        WIN = sb("WIN", [P, KD, DIN])
        CT = sb("CT", [P, KD, NE])
        normw = sb("normw", [P, KD])
        bin_ = sb("bin_", [P, KI])
        convw = sb("convw", [P, KI, TAPS])
        convb = sb("convb", [P, KI])
        ebias = sb("ebias", [P, NE])
        BR = sb("BR", [NE + 1, D])
        brow = sb("brow", [1, NSH + 1, D])
        ident = sb("ident", [P, P])
        iota = sb("iota", [P, NE])
        keep = sb("keep", [P, NT])
        mhalf = sb("mhalf", [P, 1])
        epsln = sb("epsln", [P, 1])
        epsrms = sb("epsrms", [P, 1])
        X = sb("X", [P, 2, D])
        bn = sb("bn", [P, 2, 6])
        mv = sb("mv", [P, 2, 2])
        veps = sb("veps", [P, 2])
        rstd = sb("rstd", [P, 2])
        msq = sb("msq", [P, 2])
        msqe = sb("msqe", [P, 2])
        rrms = sb("rrms", [P, 2])
        XH = sb("XH", [P, 2, 2, D])
        XT = sb("XT", [P, 2, 2 * KD, P])
        acc = sb("acc", [P, 2, D])
        uT = sb("uT", [P, 2, KI, HALO + P])
        vT = sb("vT", [P, KI, P])
        sc = sb("sc", [P, NE])
        scm = sb("scm", [P, NE])
        smax = sb("smax", [P, 1])
        ex = sb("ex", [P, NE])
        esum = sb("esum", [P, 1])
        rsum = sb("rsum", [P, 1])
        pr = sb("pr", [P, NE])
        top8 = sb("top8", [P, 8])
        idx8 = sb("idx8", [P, 8], U32)
        idxf = sb("idxf", [P, 8])
        gate1 = sb("gate1", [P, NE])
        gate2 = sb("gate2", [P, NE])
        gate = sb("gate", [P, 2, NE + 1])
        gT = sb("gT", [NE + 1, P])

        psX = pb("psX", [P, 2 * KD, P])
        psU = pb("psU", [P, KI, P])
        psV = pb("psV", [P, KI, P])
        psG = pb("psG", [P, 512])
        psS = pb("psS", [P, 512])
        psF = [pb(f"psF{n}", [P, 2, D]) for n in range(2)]

        s_passed = sem("p1_waits_passed")
        s_const = sem("p1_const_loaded")
        s_w = sem("p1_weights_loaded")
        s_wr = sem("p1_expert_weights_loaded")
        s_prep = sem("p1_weights_prepared")
        s_x = [sem(f"p1_x_loaded{q}") for q in range(2)]
        s_bn = sem("p1_bn_stats")
        s_mv = sem("p1_mean_var")
        s_pool = sem("p1_pool_steps")
        s_rstd = sem("p1_rstd")
        s_rrms = sem("p1_rrms")
        s_xn = sem("p1_xn")
        s_h = sem("p1_h")
        s_r0 = sem("p1_residual")
        s_psX = sem("p1_transposed")
        s_XT = sem("p1_XT")
        s_psU = sem("p1_projected")
        s_u = sem("p1_u")
        s_conv = sem("p1_conv_steps")
        s_halo = sem("p1_halo")
        s_psV = sem("p1_v_transposed")
        s_U = sem("p1_U_written")
        s_psG = sem("p1_scores")
        s_gs = sem("p1_gate_steps")
        s_scm = sem("p1_scores_shifted")
        s_ex = sem("p1_exp")
        s_gate = sem("p1_gate")
        s_gTps = sem("p1_gate_transposed")
        s_gT = sem("p1_gT")
        s_psS = sem("p1_shared")
        s_psF = sem("p1_expert_pair")
        s_free = sem("p1_expert_bank_free")
        s_acc = sem("p1_accumulated")
        s_st = [sem(f"p1_partial_stored{q}") for q in range(2)]

        NCONST = 11
        GSTEPS = 8
        xs, rs = t["x"], partial
        block = ctx.enter_context(nc.Block())

        @block.sync
        def _(sp):
            for dst, src in ((CT[:], t["cT"]), (normw[:], t["normw"]), (bin_[:], t["b_in"]),
                             (convw[:], t["conv_w"]), (convb[:], t["conv_b"]), (ebias[:], t["ebias"]),
                             (BR[1:NE + 1, :], t["br"]), (brow[:, 0:NSH, :], t["bs"]),
                             (brow[:, NSH, :], t["b_out"]), (ident[:], t["ident"]), (iota[:], t["iota"])):
                sp.dma_start(dst, src).then_inc(s_const, 16)

            def load(i, n, q, steady):
                if steady:
                    wait_apart(sp, s_r0, i - 1, s_passed)
                sp.dma_start(X[:, q, :], xs[bass.ts(i, P), :]).then_inc(s_x[q], 16)

            def store(i, q):
                wait_apart(sp, s_acc, (NE + 1) * (i + 1), s_passed)
                sp.dma_start(rs[bass.ts(i, P), :], acc[:, q, :]).then_inc(s_st[q], 16)

            load(0, 0, 0, False)
            sp.dma_start(WIN[:], t["win"]).then_inc(s_w, 16)
            sp.dma_start(WSraw[:], t["ws"]).then_inc(s_w, 16)
            sp.dma_start(keep[:], t["keep"]).then_inc(s_w, 16)
            load(1, 0, 1, False)
            for e in range(4):
                n = NE * D // 4
                sp.dma_start(W[:, :, e * n:(e + 1) * n], t["wr"][:, :, e * n:(e + 1) * n]).then_inc(s_wr, 16)
            with sp.Fori(0, NT // 2 - 1) as p:
                for q in range(2):
                    load(2 * p + 2 + q, p + 1, q, True)
                    store(2 * p + q, q)
            for q in range(2):
                store(NT - 2 + q, q)
            for q in range(2):
                sp.wait_ge(s_st[q], 16 * (NT // 2 + 1))

        @block.gpsimd
        def _(pool):
            nc.gpsimd.memset(epsln[:], 1e-5)
            nc.gpsimd.memset(epsrms[:], 1e-6)
            nc.gpsimd.memset(mhalf[:], -0.5).then_inc(s_pool, 1)
            pool.wait_ge(s_pool, 1)

            def stats(i, q):
                pool.wait_ge(s_mv, i + 1)
                if not isinstance(i, int) or i >= 2:
                    pool.wait_ge(s_h, i - 1)
                nc.gpsimd.tensor_tensor(veps[:, q:q + 1], mv[:, q, 1:2], epsln[:], ALU.add).then_inc(s_pool, 1)
                pool.wait_ge(s_pool, 4 * i + 2)
                nc.gpsimd.tensor_tensor(rstd[:, q:q + 1], veps[:, q:q + 1], mhalf[:], ALU.pow).then_inc(s_rstd, 1)
                pool.wait_ge(s_rstd, i + 1)
                nc.gpsimd.tensor_tensor(msq[:, q:q + 1], rstd[:, q:q + 1], rstd[:, q:q + 1], ALU.mult).then_inc(s_pool, 1)
                pool.wait_ge(s_pool, 4 * i + 3)
                nc.gpsimd.tensor_tensor(msqe[:, q:q + 1], msq[:, q:q + 1], mv[:, q, 1:2], ALU.mult).then_inc(s_pool, 1)
                pool.wait_ge(s_pool, 4 * i + 4)
                nc.gpsimd.tensor_tensor(veps[:, q:q + 1], msqe[:, q:q + 1], epsrms[:], ALU.add).then_inc(s_pool, 1)
                pool.wait_ge(s_pool, 4 * i + 5)
                nc.gpsimd.tensor_tensor(rrms[:, q:q + 1], veps[:, q:q + 1], mhalf[:], ALU.pow).then_inc(s_rrms, 1)

            stats(0, 0)
            stats(1, 1)
            with pool.Fori(1, NT // 2) as p:
                stats(2 * p, 0)
                stats(2 * p + 1, 1)

        @block.scalar
        def _(act):
            act.wait_ge(s_const, 16 * NCONST)

            def front(i, q):
                act.wait_ge(s_psX, i + 1)
                nc.scalar.activation(XT[:, q, :, :], psX[:], ACT.Copy).then_inc(s_XT, 1)
                act.wait_ge(s_psU, i + 1)
                act.wait_ge(s_halo, i + 1)
                for j in range(KI):
                    last = nc.scalar.activation(uT[:, q, j, HALO:HALO + P], psU[:, j, :], ACT.Identity,
                                                bias=bin_[:, j:j + 1])
                last.then_inc(s_u, 1)
                act.wait_ge(s_scm, i + 1)
                nc.scalar.activation(ex[:], scm[:], ACT.Exp, accum_out=esum[:]).then_inc(s_ex, 1)
                act.wait_ge(s_psV, i + 1)
                nc.scalar.activation(U[:, i, :], psV[:].rearrange("p a b -> p (a b)"), ACT.Copy).then_inc(s_U, 1)
                act.wait_ge(s_gTps, i + 1)
                nc.scalar.activation(gT[:], psG[0:NE + 1, 0:P], ACT.Copy).then_inc(s_gT, 1)

            front(0, 0)
            front(1, 1)
            with act.Fori(1, NT // 2) as p:
                front(2 * p, 0)
                front(2 * p + 1, 1)

        @block.tensor
        def _(pe):
            pe.wait_ge(s_const, 16 * NCONST)
            pe.wait_ge(s_prep, 1)

            def transposes(i, q):
                pe.wait_ge(s_h, i + 1)
                pe.wait_ge(s_XT, i)
                for j in range(2 * KD):
                    last = nc.tensor.transpose(psX[:, j, :], XH[:, q, j // KD, (j % KD) * P:(j % KD + 1) * P],
                                               ident[:])
                last.then_inc(s_psX, 1)

            def project(i, q):
                pe.wait_ge(s_XT, i + 1)
                pe.wait_ge(s_u, i)
                for j in range(KI):
                    for k in range(KD):
                        last = nc.tensor.matmul(psU[:, j, :], WIN[:, k, j * P:(j + 1) * P], XT[:, q, KD + k, :],
                                                start=(k == 0), stop=(k == KD - 1))
                last.then_inc(s_psU, 1)
                pe.wait_ge(s_gT, i)
                for k in range(KD):
                    last = nc.tensor.matmul(psG[:, 0:NE], XT[:, q, k, :], CT[:, k, :],
                                            start=(k == 0), stop=(k == KD - 1))
                last.then_inc(s_psG, 1)

            def turn(i, q):
                pe.wait_ge(s_conv, 16 * (i + 1))
                pe.wait_ge(s_U, i)
                for j in range(KI):
                    last = nc.tensor.transpose(psV[:, j, :], vT[:, j, :], ident[:])
                last.then_inc(s_psV, 1)
                pe.wait_ge(s_gate, i + 1)
                nc.tensor.transpose(psG[0:NE + 1, 0:P], gate[:, q, :], ident[:]).then_inc(s_gTps, 1)

            def pair(i, q, e):
                pe.wait_ge(s_free, PAIRS * i + e + 1)
                for k in range(KD):
                    last = nc.tensor.matmul(psF[e % 2][:].rearrange("p a b -> p (a b)"), XT[:, q, k, :],
                                            W[:, k, e * 2 * D:(e + 1) * 2 * D], start=(k == 0), stop=(k == KD - 1))
                last.then_inc(s_psF, 1)

            def shared(i, q):
                pe.wait_ge(s_gT, i + 1)
                for k in range(KD):
                    nc.tensor.matmul(psS[:, 0:D], XT[:, q, k, :], WS[:, k, :], start=(k == 0), stop=False)
                nc.tensor.matmul(psS[:, 0:D], gT[:], BR[:], start=False, stop=True).then_inc(s_psS, 1)

            def main(i, q, nxt):
                shared(i, q)
                for e in range(PAIRS):
                    pair(i, q, e)
                    if nxt is not None and e == 0:
                        transposes(*nxt)
                    if nxt is not None and e == 2:
                        project(*nxt)
                    if nxt is not None and e == PAIRS - 2:
                        turn(*nxt)

            transposes(0, 0)
            project(0, 0)
            turn(0, 0)
            pe.wait_ge(s_wr, 16 * 4)
            with pe.Fori(0, NT // 2 - 1) as p:
                main(2 * p, 0, (2 * p + 1, 1))
                main(2 * p + 1, 1, (2 * p + 2, 0))
            main(NT - 2, 0, (NT - 1, 1))
            main(NT - 1, 1, None)

        @block.vector
        def _(dve):
            dve.wait_ge(s_const, 16 * NCONST)
            dve.wait_ge(s_w, 16 * 3)
            nc.vector.tensor_tensor(brow[:, 0, :], brow[:, 0, :], brow[:, 1, :], ALU.add).then_inc(s_gs, 1)
            for k in range(KD):
                nc.vector.tensor_scalar(WIN[:, k, :], WIN[:, k, :], normw[:, k:k + 1], None, ALU.mult)
            nc.vector.tensor_tensor(WS[:], WSraw[:, :, 0, :], WSraw[:, :, 1, :], ALU.add).then_inc(s_gs, 1)
            nc.vector.memset(uT[:, 0, :, 0:HALO], 0.0).then_inc(s_halo, 1)
            dve.wait_ge(s_gs, 2)
            nc.vector.tensor_scalar(WS[:], WS[:], 1.0 / NSH, None, ALU.mult)
            nc.vector.scalar_tensor_tensor(BR[0:1, :], brow[:, 0, :], 1.0 / NSH, brow[:, NSH, :],
                                           ALU.mult, ALU.add)
            nc.vector.memset(gate[:, :, 0:1], 1.0).then_inc(s_prep, 1)
            dve.sem_inc(s_free, 2)
            for q in range(2):
                dve.sem_inc(s_st[q], 16)

            def norm(i, q, n):
                dve.wait_ge(s_x[q], 16 * n)
                nc.vector.bn_stats(bn[:, q, :], X[:, q, :]).then_inc(s_bn, 1)
                wait_apart(dve, s_bn, i + 1, s_passed)
                nc.vector.bn_aggr(mv[:, q, :], bn[:, q, :]).then_inc(s_mv, 1)

            def apply(i, q):
                dve.wait_ge(s_mv, i + 1)
                dve.wait_ge(s_rstd, i + 1)
                nc.vector.tensor_scalar(XH[:, q, 0, :], X[:, q, :], mv[:, q, 0:1], rstd[:, q:q + 1],
                                        ALU.subtract, ALU.mult).then_inc(s_xn, 1)
                dve.wait_ge(s_xn, i + 1)
                dve.wait_ge(s_rrms, i + 1)
                nc.vector.tensor_scalar(XH[:, q, 1, :], XH[:, q, 0, :], rrms[:, q:q + 1], None,
                                        ALU.mult).then_inc(s_h, 1)

            def residual(i, q):
                dve.wait_ge(s_st[q], 16 * ((i - q) // 2 + 1) if isinstance(i, int) else 8 * (i - q) + 16)
                nc.vector.scalar_tensor_tensor(acc[:, q, :], XH[:, q, 0, :], 2.0, X[:, q, :],
                                               ALU.mult, ALU.add).then_inc(s_r0, 1)

            def scores(i, q):
                b = GSTEPS * i + 2
                dve.wait_ge(s_psG, i + 1)
                nc.vector.tensor_tensor(sc[:], psG[:, 0:NE], ebias[:], ALU.add).then_inc(s_gs, 1)
                dve.wait_ge(s_gs, b + 1)
                nc.vector.reduce_max(smax[:], sc[:], AX.X).then_inc(s_gs, 1)
                dve.wait_ge(s_gs, b + 2)
                nc.vector.tensor_scalar(scm[:], sc[:], smax[:], None, ALU.subtract).then_inc(s_scm, 1)

            def gates(i, q):
                b = GSTEPS * i + 4
                dve.wait_ge(s_ex, i + 1)
                nc.vector.reciprocal(rsum[:], esum[:]).then_inc(s_gs, 1)
                dve.wait_ge(s_gs, b + 1)
                nc.vector.tensor_scalar(pr[:], ex[:], rsum[:], None, ALU.mult).then_inc(s_gs, 1)
                wait_apart(dve, s_gs, b + 2, s_passed)
                nc.vector.max(top8[:], pr[:]).then_inc(s_gs, 1)
                wait_apart(dve, s_gs, b + 3, s_passed)
                nc.vector.max_index(idx8[:], top8[:], pr[:]).then_inc(s_gs, 1)
                dve.wait_ge(s_gs, b + 4)
                nc.vector.tensor_copy(idxf[:], idx8[:]).then_inc(s_gs, 1)
                dve.wait_ge(s_gs, b + 5)
                nc.vector.scalar_tensor_tensor(gate1[:], iota[:], idxf[:, 0:1], pr[:], ALU.is_equal, ALU.mult)
                nc.vector.scalar_tensor_tensor(gate2[:], iota[:], idxf[:, 1:2], pr[:], ALU.is_equal,
                                               ALU.mult).then_inc(s_gs, 1)
                dve.wait_ge(s_gs, b + 6)
                nc.vector.tensor_tensor(gate[:, q, 1:NE + 1], gate1[:], gate2[:], ALU.add).then_inc(s_gate, 1)

            def conv(i, q, nxt_halo):
                dve.wait_ge(s_u, i + 1)
                if not isinstance(i, int) or i >= 1:
                    dve.wait_ge(s_psV, i)
                for k in range(TAPS):
                    for j in range(KI):
                        src, w = uT[:, q, j, k:k + P], convw[:, j, k:k + 1]
                        if k == 0:
                            op = nc.vector.tensor_scalar(vT[:, j, :], src, w, convb[:, j:j + 1], ALU.mult, ALU.add)
                        else:
                            dve.wait_ge(s_conv, 16 * i + 4 * (k - 1) + j + 1)
                            op = nc.vector.scalar_tensor_tensor(vT[:, j, :], src, w, vT[:, j, :], ALU.mult, ALU.add)
                        op.then_inc(s_conv, 1)
                if nxt_halo is not None:
                    nc.vector.tensor_scalar(uT[:, 1 - q, :, 0:HALO], uT[:, q, :, P:P + HALO],
                                            keep[:, nxt_halo], None, ALU.mult).then_inc(s_halo, 1)

            def experts(i, q, pairs):
                for e in pairs:
                    dve.wait_ge(s_psF, PAIRS * i + e + 1)
                    for a in range(2):
                        n = (NE + 1) * i + 2 * e + a + 1
                        dve.wait_ge(s_acc, n)
                        op = nc.vector.scalar_tensor_tensor(
                            acc[:, q, :], psF[e % 2][:, a, :], gate[:, q, 1 + 2 * e + a:2 + 2 * e + a],
                            acc[:, q, :], ALU.mult, ALU.add).then_inc(s_acc, 1)
                    dve.wait_ge(s_acc, n + 1)
                    dve.sem_inc(s_free, 1)

            def main(i, q, nxt):
                if nxt is not None:
                    ni, nq, n = nxt
                    norm(ni, nq, n)
                dve.wait_ge(s_psS, i + 1)
                dve.wait_ge(s_r0, i + 1)
                nc.vector.tensor_tensor(acc[:, q, :], psS[:, 0:D], acc[:, q, :], ALU.add).then_inc(s_acc, 1)
                if nxt is not None:
                    apply(ni, nq)
                experts(i, q, (0, 1))
                if nxt is not None:
                    residual(ni, nq)
                experts(i, q, (2, 3))
                if nxt is not None:
                    scores(ni, nq)
                experts(i, q, (4,))
                if nxt is not None:
                    gates(ni, nq)
                experts(i, q, (5,))
                if nxt is not None:
                    conv(ni, nq, None if isinstance(ni, int) and ni == NT - 1 else
                         (slice(ni + 1, ni + 2) if isinstance(ni, int) else bass.ds(ni + 1, 1)))
                experts(i, q, (6, 7))

            norm(0, 0, 1)
            apply(0, 0)
            residual(0, 0)
            scores(0, 0)
            gates(0, 0)
            conv(0, 0, slice(1, 2))
            with dve.Fori(0, NT // 2 - 1) as p:
                main(2 * p, 0, (2 * p + 1, 1, p + 1))
                main(2 * p + 1, 1, (2 * p + 2, 0, p + 2))
            main(NT - 2, 0, (NT - 1, 1, NT // 2))
            main(NT - 1, 1, None)


def phase2(nc, t, U, table):
    ctx = ExitStack()
    with ctx:
        def sb(name, shape, dt=F32):
            return ctx.enter_context(nc.sbuf_tensor(name, shape, dt))

        def pb(name, shape, dt=F32):
            return ctx.enter_context(nc.psum_tensor(name, shape, dt))

        def sem(name):
            return ctx.enter_context(nc.semaphore(name))

        A1 = sb("A1", [P, NG, NST])
        A1T = sb("A1T", [P, NG, NST])
        Bv = sb("Bv", [P, NG])
        Cv = sb("Cv", [P, NG])
        own = sb("own", [P, CG])
        ident = sb("ident2", [P, P])
        zero = sb("zero", [NG, (P - 1) * CG])
        Dm = sb("Dm", [P, GB, P])
        DTm = sb("DTm", [P, GB, P])
        D128 = sb("D128", [P, 2, GB, P])
        XR = sb("XR", [P, GB, P + NST])
        YR = sb("YR", [P, 2, GB, P + 1 + NST])
        Bblk = sb("Bblk", [P, GB, CG])
        KT = sb("KT", [P, GB, CG])
        QG = sb("QG", [P, 2, GB, P])
        TO = sb("TO", [P, GB, P, CG])
        US = sb("US", [P, CB, NT])
        QS = sb("QS", [NT, GB, P])
        q0 = sb("q0", [P, GB, BATCH, NCH])
        H = sb("H", [P, GB, BATCH, NCH])
        HM = sb("HM", [P, 2, CG, NT])

        psA = pb("psA", [P, GB, P])
        psB = pb("psB", [P, GB, P])
        psK = pb("psK", [P, GB, P])
        psQ = pb("psQ", [NT, GB, P])
        psR = pb("psR", [P, GB, NT])
        psT = [pb(f"psT{n}", [P, CG, NT]) for n in range(2)]

        s_passed = sem("p2_waits_passed")
        s_c = sem("p2_const")
        s_zero = sem("p2_zero")
        s_tz = sem("p2_table_zeroed")
        s_init = sem("p2_block_start")
        s_initd = sem("p2_block_start_diagonal")
        s_y1 = sem("p2_first_step")
        s_y1c = sem("p2_first_step_copied")
        s_lev = sem("p2_level_done")
        s_cp = sem("p2_level_copied")
        s_dg = sem("p2_level_diagonal")
        s_dgt = sem("p2_level_diagonal_t")
        s_psK = sem("p2_impulse")
        s_KT = sem("p2_impulse_copied")
        s_kst = sem("p2_impulse_stored")
        s_qgp = sem("p2_qg_transposed")
        s_QG = sem("p2_QG")
        s_TO = sem("p2_toeplitz")
        s_US = sem("p2_US")
        s_psQ = sem("p2_state_input")
        s_QS = sem("p2_state_input_copied")
        s_qT = sem("p2_state_input_turned")
        s_q0 = sem("p2_q0")
        s_rec = sem("p2_recurrence")
        s_H = sem("p2_state")
        s_HM = sem("p2_state_spread")
        s_T = sem("p2_chunk_out")
        s_Uo = sem("p2_out_written")

        to_elem = CG
        block = ctx.enter_context(nc.Block())
        NCONST = 6

        @block.sync
        def _(sp):
            for dst, src in ((A1[:], t["A"]), (A1T[:], t["AT"]), (Bv[:], t["B"]), (Cv[:], t["C"]),
                             (own[:], t["own"]), (ident[:], t["ident"])):
                sp.dma_start(dst, src).then_inc(s_c, 16)
            sp.wait_ge(s_zero, 1)
            sp.dma_start(bass.AP(table, P * CG, [[TROWS * CG, NG], [1, (P - 1) * CG]]), zero[:]).then_inc(s_tz, 16)
            sp.wait_ge(s_tz, 16)

            def put(k):
                wait_apart(sp, s_KT, k + 1, s_passed)
                sp.dma_start(bass.AP(table, k * (GB * TROWS * CG), [[CG, P], [TROWS * CG, GB], [1, CG]]),
                             KT[:]).then_inc(s_kst, 16)

            def get(k):
                wait_apart(sp, s_kst, 16 * (k + 1), s_passed)
                wait_apart(sp, s_T, GB * k, s_passed)
                for j in range(GB):
                    sp.dma_start(TO[:, j, :, :], bass.AP(table, k * (GB * TROWS * CG) + j * TROWS * CG,
                                                         [[CG, P], [1, P * CG]])).then_inc(s_TO, 16)

            put(0)
            get(0)
            with sp.Fori(1, NB) as k:
                put(k)
                get(k)
            sp.wait_ge(s_TO, 16 * GB * NB)

        def spread(eng, out, compact, j):
            return eng.tensor_tensor(out[:, j, :].rearrange("p (c s) -> p c s", c=CG),
                                     compact.unsqueeze(1).to_broadcast([P, CG, NST]),
                                     own[:].unsqueeze(2).to_broadcast([P, CG, NST]), ALU.mult)

        @block.gpsimd
        def _(pool):
            nc.gpsimd.memset(zero[:], 0.0).then_inc(s_zero, 1)
            pool.wait_ge(s_c, 16 * NCONST)

            def prep(k):
                pool.wait_ge(s_lev, LEVELS * k)
                for j in range(GB):
                    last = spread(nc.gpsimd, DTm, A1T[:, k * GB + j, :], j)
                last.then_inc(s_initd, 1)

            def level(k, n):
                if n == LEVELS - 1:
                    return
                pool.wait_ge(s_cp, LEVELS * k + n + 1)
                for j in range(GB):
                    last = spread(nc.gpsimd, DTm, XR[:, j, P:P + NST], j)
                last.then_inc(s_dgt, 1)

            def gather(k):
                pool.wait_ge(s_psQ, k)
                pool.wait_ge(s_T, GB * k)
                src = U[:, :, bass.ds(k * CB, CB)] if not isinstance(k, int) else U[:, :, k * CB:(k + 1) * CB]
                nc.gpsimd.tensor_copy(US[:], src.rearrange("p n d -> p d n")).then_inc(s_US, 1)

            def mask(k, j):
                if not isinstance(k, int) or GB * k + j >= 2:
                    pool.wait_ge(s_T, GB * k + j - 1)
                nc.gpsimd.tensor_tensor(HM[:, j % 2, :, :],
                                        H[:, j, :, :].rearrange("p b c -> p (b c)").unsqueeze(1).to_broadcast([P, CG, NT]),
                                        own[:].unsqueeze(2).to_broadcast([P, CG, NT]), ALU.mult).then_inc(s_HM, 1)

            prep(0)
            for n in range(LEVELS):
                level(0, n)
            gather(0)

            def body(k, more):
                if more:
                    prep(k + 1)
                    for n in range(LEVELS):
                        level(k + 1, n)
                pool.wait_ge(s_H, NCH * (k + 1))
                for j in range(GB):
                    mask(k, j)
                if more:
                    gather(k + 1)

            body(0, True)
            with pool.Fori(1, NB - 1) as k:
                body(k, True)
            body(NB - 1, False)

        @block.tensor
        def _(pe):
            pe.wait_ge(s_c, 16 * NCONST)

            def first(k, q):
                pe.wait_ge(s_init, k + 1)
                pe.wait_ge(s_initd, k + 1)
                for j in range(GB):
                    last = nc.tensor.matmul(psB[:, j, 0:1], DTm[:, j, :], YR[:, q, j, P:P + 1], start=True, stop=True)
                last.then_inc(s_y1, 1)

            def level(k, q, n):
                m = 1 << n
                if n == 0:
                    pe.wait_ge(s_y1c, k + 1)
                else:
                    pe.wait_ge(s_dg, LEVELS * k + n)
                    pe.wait_ge(s_dgt, (LEVELS - 1) * k + n)
                for j in range(GB):
                    nc.tensor.matmul(psA[:, j, 0:m + NST], Dm[:, j, :], XR[:, j, P - m:P + NST], start=True, stop=True)
                for j in range(GB):
                    last = nc.tensor.matmul(psB[:, j, 0:m + 1 + NST],
                                            DTm[:, j, :], YR[:, q, j, P - m:P + 1 + NST], start=True, stop=True)
                last.then_inc(s_lev, 1)

            def finish(k, q):
                pe.wait_ge(s_cp, LEVELS * (k + 1))
                pe.wait_ge(s_QG, k)
                for j in range(GB):
                    last = nc.tensor.matmul(psK[:, j, 0:CG], YR[:, q, j, 1:P + 1], Bblk[:, j, :], start=True, stop=True)
                last.then_inc(s_psK, 1)
                pe.wait_ge(s_KT, k + 1)
                for j in range(GB):
                    last = nc.tensor.transpose(psK[:, j, :], XR[:, j, 0:P], ident[:])
                last.then_inc(s_qgp, 1)

            def state_input(k, q):
                pe.wait_ge(s_US, k + 1)
                pe.wait_ge(s_QG, k + 1)
                pe.wait_ge(s_QS, k)
                for c in range(CB):
                    j, e = c // CG, c % CG
                    last = nc.tensor.matmul(psQ[:, j, e * NST:(e + 1) * NST], US[:, c, :],
                                            QG[:, q, j, e * NST:(e + 1) * NST], start=True, stop=True)
                last.then_inc(s_psQ, 1)
                wait_apart(pe, s_QS, k + 1, s_passed)
                for j in range(GB):
                    last = nc.tensor.transpose(psR[:, j, :], QS[:, j, :], ident[0:NT, 0:NT])
                last.then_inc(s_qT, 1)

            def step(k, q, c):
                pe.wait_ge(s_H, NCH * k + c + 1)
                if c == 0:
                    pe.wait_ge(s_q0, k + 1)
                for j in range(GB):
                    last = nc.tensor.matmul(psR[:, j, 0:BATCH], D128[:, q, j, :], H[:, j, :, c], start=True, stop=True)
                last.then_inc(s_rec, 1)

            def outputs(k, q, j):
                n = GB * k + j
                if not isinstance(k, int) or n >= 2:
                    pe.wait_ge(s_Uo, n - 1)
                if j == 0:
                    pe.wait_ge(s_TO, 16 * GB * (k + 1))
                for e in range(CG):
                    nc.tensor.matmul(psT[j % 2][:, e, :], TO[:, j, :, e], US[:, j * CG + e, :],
                                     start=(e == 0), stop=False, skip_group_check=True)
                pe.wait_ge(s_HM, n + 1)
                nc.tensor.matmul(psT[j % 2][:].rearrange("p e n -> p (e n)"), YR[:, q, j, 0:P],
                                 HM[:, j % 2, :, :].rearrange("p e n -> p (e n)"),
                                 start=False, stop=True, skip_group_check=True).then_inc(s_T, 1)

            def body(k, q, more):
                if more:
                    first(k + 1, 1 - q)
                state_input(k, q)
                for c in range(LEVELS):
                    if more:
                        level(k + 1, 1 - q, c)
                    step(k, q, c)
                if more:
                    finish(k + 1, 1 - q)
                for j in range(GB):
                    outputs(k, q, j)

            first(0, 0)
            for n in range(LEVELS):
                level(0, 0, n)
            finish(0, 0)
            body(0, 0, True)
            with pe.Fori(0, NB // 2 - 1) as h:
                body(2 * h + 1, 1, True)
                body(2 * h + 2, 0, True)
            body(NB - 1, 1, False)

        @block.vector
        def _(dve):
            dve.wait_ge(s_c, 16 * NCONST)

            def start(k, q):
                g = slice(GB * k, GB * (k + 1)) if isinstance(k, int) else bass.ds(GB * k, GB)
                dve.wait_ge(s_qgp, k)
                if not isinstance(k, int) or k >= 2:
                    dve.wait_ge(s_T, GB * (k - 1))
                nc.vector.tensor_copy(XR[:, :, P - 1], Bv[:, g])
                nc.vector.tensor_copy(XR[:, :, P:P + NST], A1T[:, g, :])
                nc.vector.tensor_copy(YR[:, q, :, P], Cv[:, g])
                nc.vector.tensor_copy(YR[:, q, :, P + 1:P + 1 + NST], A1[:, g, :])
                for j in range(GB):
                    gj = GB * k + j
                    spread(nc.vector, Dm, A1[:, gj, :], j)
                    last = nc.vector.tensor_tensor(Bblk[:, j, :], own[:],
                                                   Bv[:, gj:gj + 1].to_broadcast([P, CG]) if isinstance(k, int)
                                                   else Bv[:, bass.ds(gj, 1)].to_broadcast([P, CG]), ALU.mult)
                last.then_inc(s_init, 1)

            def first(k, q):
                dve.wait_ge(s_y1, k + 1)
                nc.vector.tensor_copy(YR[:, q, :, P - 1], psB[:, :, 0]).then_inc(s_y1c, 1)

            def level(k, q, n):
                m = 1 << n
                dve.wait_ge(s_lev, LEVELS * k + n + 1)
                nc.vector.tensor_copy(XR[:, :, P - 2 * m:P - m], psA[:, :, 0:m])
                nc.vector.tensor_copy(XR[:, :, P:P + NST], psA[:, :, m:m + NST])
                nc.vector.tensor_copy(YR[:, q, :, P + 1:P + 1 + NST], psB[:, :, m + 1:m + 1 + NST])
                nc.vector.tensor_copy(YR[:, q, :, P - 2 * m:P - m], psB[:, :, 0:m]).then_inc(s_cp, 1)
                dve.wait_ge(s_cp, LEVELS * k + n + 1)
                for j in range(GB):
                    last = spread(nc.vector, Dm if n < LEVELS - 1 else D128[:, q, :, :],
                                  YR[:, q, j, P + 1:P + 1 + NST], j)
                last.then_inc(s_dg, 1)

            def seed(k, q):
                dve.wait_ge(s_q0, k + 1)
                nc.vector.tensor_copy(H[:, :, :, 1], q0[:, :, :, 0]).then_inc(s_H, 1)

            def step(k, q, c):
                dve.wait_ge(s_rec, LEVELS * k + c + 1)
                nc.vector.tensor_tensor(H[:, :, :, c + 1], psR[:, :, 0:BATCH], q0[:, :, :, c], ALU.add).then_inc(s_H, 1)

            start(0, 0)
            first(0, 0)
            for n in range(LEVELS):
                level(0, 0, n)

            def body(k, q, more):
                if more:
                    start(k + 1, 1 - q)
                    first(k + 1, 1 - q)
                dve.wait_ge(s_HM, GB * k)
                nc.vector.memset(H[:, :, :, 0], 0.0).then_inc(s_H, 1)
                for c in range(LEVELS):
                    if more:
                        level(k + 1, 1 - q, c)
                    step(k, q, c)

            body(0, 0, True)
            with dve.Fori(0, NB // 2 - 1) as h:
                body(2 * h + 1, 1, True)
                body(2 * h + 2, 0, True)
            body(NB - 1, 1, False)

        @block.scalar
        def _(act):
            def finish(k, q):
                act.wait_ge(s_psK, k + 1)
                act.wait_ge(s_kst, 16 * k)
                nc.scalar.activation(KT[:], psK[:, :, 0:CG], ACT.Copy).then_inc(s_KT, 1)
                act.wait_ge(s_qgp, k + 1)
                nc.scalar.activation(QG[:, q, :, :], psK[:], ACT.Copy).then_inc(s_QG, 1)

            def body(k, q, more):
                act.wait_ge(s_psQ, k + 1)
                nc.scalar.activation(QS[:], psQ[:], ACT.Copy).then_inc(s_QS, 1)
                act.wait_ge(s_qT, k + 1)
                nc.scalar.activation(q0[:].rearrange("p j b c -> p j (b c)"), psR[:], ACT.Copy).then_inc(s_q0, 1)
                if more:
                    finish(k + 1, 1 - q)
                for j in range(GB):
                    act.wait_ge(s_T, GB * k + j + 1)
                    d0 = CB * k + CG * j
                    dst = U[:, :, d0:d0 + CG] if isinstance(k, int) else U[:, :, bass.ds(d0, CG)]
                    nc.scalar.activation(dst.rearrange("p n e -> p e n"), psT[j % 2][:], ACT.Copy).then_inc(s_Uo, 1)

            finish(0, 0)
            body(0, 0, True)
            with act.Fori(0, NB // 2 - 1) as h:
                body(2 * h + 1, 1, True)
                body(2 * h + 2, 0, True)
            body(NB - 1, 1, False)


def phase3(nc, t, U, partial, out):
    ctx = ExitStack()
    with ctx:
        def sb(name, shape, dt=F32):
            return ctx.enter_context(nc.sbuf_tensor(name, shape, dt))

        def pb(name, shape, dt=F32):
            return ctx.enter_context(nc.psum_tensor(name, shape, dt))

        def sem(name):
            return ctx.enter_context(nc.semaphore(name))

        NBUF = 4
        WO = sb("WO", [P, KI, D])
        ident = sb("ident3", [P, P])
        Y = sb("Y", [P, 2, DIN])
        YT = sb("YT", [P, 2, KI, P])
        R = sb("R", [P, NBUF, D])
        O = sb("O", [P, NBUF, D])
        psY = [pb(f"psY{n}", [P, KI, P]) for n in range(2)]
        psO = [pb(f"psO{n}", [P, 512]) for n in range(2)]
        s_passed = sem("p3_waits_passed")
        s_c = sem("p3_const")
        s_Y = sem("p3_y_staged")
        s_psY = sem("p3_y_transposed")
        s_YT = sem("p3_YT")
        s_psO = sem("p3_projected")
        s_O = sem("p3_summed")
        s_R = [sem(f"p3_partial_loaded{n}") for n in range(NBUF)]
        s_out = [sem(f"p3_stored{n}") for n in range(NBUF)]
        block = ctx.enter_context(nc.Block())

        @block.sync
        def _(sp):
            sp.dma_start(WO[:], t["wout"]).then_inc(s_c, 16)
            sp.dma_start(ident[:], t["ident"]).then_inc(s_c, 16)
            sp.wait_ge(s_c, 32)
            for q in range(NBUF):
                sp.dma_start(R[:, q, :], partial[bass.ts(q, P), :]).then_inc(s_R[q], 16)
            with sp.Fori(1, NT // NBUF) as p:
                for q in range(NBUF):
                    i = NBUF * p + q
                    wait_apart(sp, s_O, i - NBUF + 1, s_passed)
                    sp.dma_start(R[:, q, :], partial[bass.ts(i, P), :]).then_inc(s_R[q], 16)

        @block.gpsimd
        def _(pool):
            def stage(i, q):
                if not isinstance(i, int) or i >= 2:
                    pool.wait_ge(s_psY, i - 1)
                nc.gpsimd.tensor_copy(Y[:, q, :], U[:, i, :]).then_inc(s_Y, 1)
            stage(0, 0)
            stage(1, 1)
            with pool.Fori(1, NT // 2) as p:
                stage(2 * p, 0)
                stage(2 * p + 1, 1)

        @block.tensor
        def _(pe):
            pe.wait_ge(s_c, 32)

            def turn(i, q):
                pe.wait_ge(s_Y, i + 1)
                if not isinstance(i, int) or i >= 2:
                    pe.wait_ge(s_YT, i - 1)
                for j in range(KI):
                    last = nc.tensor.transpose(psY[q][:, j, :], Y[:, q, j * P:(j + 1) * P], ident[:])
                last.then_inc(s_psY, 1)

            def project(i, q):
                pe.wait_ge(s_YT, i + 1)
                if not isinstance(i, int) or i >= 2:
                    pe.wait_ge(s_O, i - 1)
                for j in range(KI):
                    last = nc.tensor.matmul(psO[q][:, 0:D], YT[:, q, j, :], WO[:, j, :], start=(j == 0), stop=(j == KI - 1))
                last.then_inc(s_psO, 1)

            turn(0, 0)
            turn(1, 1)
            project(0, 0)
            with pe.Fori(1, NT // 2) as p:
                turn(2 * p, 0)
                project(2 * p - 1, 1)
                turn(2 * p + 1, 1)
                project(2 * p, 0)
            project(NT - 1, 1)

        @block.scalar
        def _(act):
            def copy(i, q):
                act.wait_ge(s_psY, i + 1)
                if not isinstance(i, int) or i >= 2:
                    act.wait_ge(s_psO, i - 1)
                nc.scalar.activation(YT[:, q, :, ::-1], psY[q][:], ACT.Copy).then_inc(s_YT, 1)

            def store(i, q):
                act.wait_ge(s_O, i + 1)
                act.dma_start(out[bass.ts(i, P), :], O[:, q, :]).then_inc(s_out[q], 16)

            copy(0, 0)
            copy(1, 1)
            copy(2, 0)
            copy(3, 1)
            with act.Fori(1, NT // NBUF) as p:
                for q in range(NBUF):
                    copy(NBUF * p + q, q % 2)
                    store(NBUF * p + q - NBUF, q)
            for q in range(NBUF):
                store(NT - NBUF + q, q)
            for q in range(NBUF):
                act.wait_ge(s_out[q], 16 * (NT // NBUF))

        @block.vector
        def _(dve):
            def add(i, q, n):
                dve.wait_ge(s_psO, i + 1)
                dve.wait_ge(s_R[q], 16 * n + 16)
                if not isinstance(n, int):
                    dve.wait_ge(s_out[q], 16 * n)
                nc.vector.tensor_tensor(O[:, q, :], psO[q % 2][:, 0:D], R[:, q, :], ALU.add).then_inc(s_O, 1)
            for q in range(NBUF):
                add(q, q, 0)
            with dve.Fori(1, NT // NBUF) as p:
                for q in range(NBUF):
                    add(NBUF * p + q, q, p)


def program(nc, t, out):
    partial = nc.dram_tensor("partial", [NTOK, D], F32, kind="Internal")
    table = nc.dram_tensor("responses", [NG, TROWS, CG], F32, kind="Internal")
    with nc.sbuf_tensor("U", [P, NT, DIN], F32) as U:
        phase1(nc, t, U, partial)
        phase2(nc, t, U, table)
        phase3(nc, t, U, partial, out)


def kernel(L0_attn_x, L0_attn_norm_w, L0_attn_Win, L0_attn_b_in, L0_attn_conv_w, L0_attn_conv_b, L0_attn_A,
           L0_attn_Bm, L0_attn_Cm, L0_attn_Wout, L0_attn_b_out, L0_ffn_centroids, L0_ffn_expert_biases,
           L0_ffn_Wr, L0_ffn_br, L0_ffn_Ws, L0_ffn_bs):
    import concourse.bacc as bacc
    from concourse.bass_utils import run_bass_kernel_spmd

    def a(v):
        return np.asarray(v)

    def blocks(v, k):
        v = a(v)
        return v.reshape((k, P) + v.shape[1:]).swapaxes(0, 1)

    A = a(L0_attn_A)
    arrays = {
        "x": a(L0_attn_x).reshape(NTOK, D),
        "normw": blocks(L0_attn_norm_w, KD),
        "win": blocks(L0_attn_Win, KD),
        "b_in": blocks(L0_attn_b_in, KI),
        "conv_w": blocks(a(L0_attn_conv_w)[:, 0, :], KI),
        "conv_b": blocks(L0_attn_conv_b, KI),
        "A": A.reshape(NG, P, NST).transpose(1, 0, 2),
        "AT": A.transpose(0, 2, 1).reshape(NG, P, NST).transpose(1, 0, 2),
        "B": a(L0_attn_Bm).reshape(NG, P).T,
        "C": a(L0_attn_Cm).reshape(NG, P).T,
        "wout": blocks(L0_attn_Wout, KI),
        "b_out": a(L0_attn_b_out).reshape(1, D),
        "cT": blocks(a(L0_ffn_centroids).T, KD),
        "ebias": np.broadcast_to(a(L0_ffn_expert_biases)[None, :], (P, NE)),
        "wr": blocks(a(L0_ffn_Wr).transpose(2, 0, 1).reshape(D, NE * D), KD),
        "br": a(L0_ffn_br),
        "ws": blocks(a(L0_ffn_Ws).transpose(2, 0, 1), KD),
        "bs": a(L0_ffn_bs).reshape(1, NSH, D),
        "ident": np.eye(P, dtype=np.float32),
        "iota": np.tile(np.arange(NE, dtype=np.float32), (P, 1)),
        "keep": np.tile((np.arange(NT) % NCH != 0).astype(np.float32), (P, 1)),
        "own": (np.arange(P)[:, None] // NST == np.arange(CG)[None, :]).astype(np.float32),
    }
    nc = bacc.Bacc("TRN2", target_bir_lowering=False, num_devices=1)
    arrays = {f"in_{n}": np.ascontiguousarray(v) for n, v in arrays.items()}
    t = {n[3:]: nc.dram_tensor(n, v.shape, F32, kind="ExternalInput").ap() for n, v in arrays.items()}
    out = nc.dram_tensor("out_0", (NTOK, D), F32, kind="ExternalOutput").ap()
    program(nc, t, out)
    r = run_bass_kernel_spmd(nc, [arrays], core_ids=[0])
    return r.results[0]["out_0"].reshape(BATCH, SEQ, D)
```

```python
import numpy as np
import concourse.bass as bass
from concourse import mybir
from contextlib import ExitStack

F32 = mybir.dt.float32
BF16 = mybir.dt.bfloat16
U32 = mybir.dt.uint32
I32 = mybir.dt.int32
ALU = mybir.AluOpType
ACT = mybir.ActivationFunctionType
AX = mybir.AxisListType

P = 128
BATCH, SEQ, D = 8, 1024, 256
DIN, NST, TAPS = 512, 16, 4
NE, NSH, TOPK = 16, 2, 2
NTOK = BATCH * SEQ
NT = NTOK // P
NCH = SEQ // P
KD = D // P
KI = DIN // P
CG = P // NST
NG = DIN // CG
GB = 4
NB = NG // GB
CB = CG * GB
HALO = TAPS - 1
NX = TOPK * NT + NE
REG = NTOK + P
LEVELS = 7
WIDE = 64
TROWS = 2 * P - 1


def at(i):
    return slice(i, i + 1) if isinstance(i, int) else bass.ds(i, 1)


def wait_apart(eng, sem, value, passed):
    eng.wait_ge(sem, value)
    eng.sem_inc(passed, 1)


def phase1(nc, t, U, route, partial, rows):
    ctx = ExitStack()
    with ctx:
        def sb(name, shape, dt=F32):
            return ctx.enter_context(nc.sbuf_tensor(name, shape, dt))

        def pb(name, shape, dt=F32):
            return ctx.enter_context(nc.psum_tensor(name, shape, dt))

        def sem(name):
            return ctx.enter_context(nc.semaphore(name))

        POS, TOPV, TAB = route
        R = 4
        WS = sb("WS", [P, KD, D])
        WSraw = sb("WSraw", [P, KD, NSH, D])
        WIN = sb("WIN", [P, KD, DIN])
        CT = sb("CT", [P, KD, NE])
        normw = sb("normw", [P, KD])
        bin_ = sb("bin_", [P, KI])
        convw = sb("convw", [P, KI, TAPS])
        convb = sb("convb", [P, DIN])
        taps = sb("taps", [P, KI, TAPS, P])
        ebias = sb("ebias", [P, NE])
        BR = sb("BR", [NE + 1, D])
        brow = sb("brow", [1, NSH + 1, D])
        ident = sb("ident", [P, P])
        before = sb("before", [P, P])
        ones = sb("ones", [P, P], BF16)
        iota = sb("iota", [P, NE])
        down = sb("down", [P, 1])
        keep = sb("keep", [P, NT])
        tileno = sb("tileno", [1, NX])
        mhalf = sb("mhalf", [P, 1])
        epsln = sb("epsln", [P, 1])
        epsrms = sb("epsrms", [P, 1])
        zero = sb("zero1", [P, D])
        X = sb("X", [P, R, D])
        bn = sb("bn", [P, R, 6])
        mv = sb("mv", [P, R, 2])
        veps = sb("veps", [P, R])
        rstd = sb("rstd", [P, R])
        msq = sb("msq", [P, R])
        msqe = sb("msqe", [P, R])
        rrms = sb("rrms", [P, R])
        XN = sb("XN", [P, R, D])
        HN = sb("HN", [P, 2, D])
        XT = sb("XT", [P, 2, 2 * KD, P])
        acc = sb("acc", [P, R, D])
        uT = sb("uT", [P, 2, KI, HALO + P])
        sc = sb("sc", [P, NE])
        scm = sb("scm", [P, NE])
        smax = sb("smax", [P, 1])
        ex = sb("ex", [P, NE])
        esum = sb("esum", [P, 1])
        rsum = sb("rsum", [P, 1])
        pr = sb("pr", [P, NE])
        top8 = sb("top8", [P, 8])
        idx8 = sb("idx8", [P, 8], U32)
        idxf = sb("idxf", [P, 2, 8])
        one1 = sb("one1", [P, NE])
        mask = sb("mask", [P, 2, NE], BF16)
        before16 = sb("before16", [P, P], BF16)
        gate = sb("gate", [P, 2, NE + 1])
        gT = sb("gT", [NE + 1, P])
        nxt = sb("nxt", [P, 2, NE])
        place = sb("place", [P, 2, NE])
        spare_out = sb("spare_out", [P, 2, NE])
        posf = sb("posf", [P, 2, TOPK])
        posu = sb("posu", [P, R, TOPK], U32)
        tail = sb("tail", [P, NE])
        tailu = sb("tailu", [P, NE, 1], U32)
        IDX = sb("IDX", [P, NT, TOPK])
        PF = sb("PF", [P, NT, TOPK])
        used = sb("used", [P, 3, NE])
        usedi = sb("usedi", [P, 2, NE], I32)
        ends = sb("ends", [P, 2, NE])
        shift = sb("shift", [P, 2, NE])
        hit = WSraw[:].rearrange("p k s d -> p (k s d)").rearrange("p (n e) -> p n e", e=NE)
        moved = sb("moved", [P, 2, NT, TOPK])
        ge = sb("ge", [1, NX, NE])
        geb = sb("geb", [1, NX, NE])
        own_ = sb("own_", [1, 4, NX])

        psX = pb("psX", [P, 2 * KD, P])
        psU = pb("psU", [P, KI, P])
        psV = pb("psV", [P, KI, P])
        psG = pb("psG", [P, 512])
        psK = pb("psRank", [P, 512])
        psT = pb("psGT", [P, 512])
        psS = pb("psS", [P, 512])

        s_passed = sem("p1_waits_passed")
        s_const = sem("p1_const_loaded")
        s_w = sem("p1_weights_loaded")
        s_prep = sem("p1_weights_prepared")
        s_x = [sem(f"p1_x_loaded{r}") for r in range(R)]
        s_bn = sem("p1_bn_stats")
        s_mv = sem("p1_mean_var")
        s_pool = sem("p1_pool_steps")
        s_rstd = sem("p1_rstd")
        s_rrms = sem("p1_rrms")
        s_xn = sem("p1_xn")
        s_h = sem("p1_h")
        s_r0 = sem("p1_residual")
        s_psX = sem("p1_transposed")
        s_XT = sem("p1_XT")
        s_psU = sem("p1_projected")
        s_u = sem("p1_u")
        s_halo = sem("p1_halo")
        s_psV = sem("p1_convolved")
        s_U = sem("p1_U_written")
        s_psG = sem("p1_scores")
        s_gs = sem("p1_gate_steps")
        s_scm = sem("p1_scores_shifted")
        s_ex = sem("p1_exp")
        s_gate = sem("p1_gate")
        s_rank = sem("p1_ranks")
        s_place = sem("p1_places")
        s_mask = sem("p1_mask")
        s_pf = sem("p1_positions_summed")
        s_pos = sem("p1_positions")
        s_gTps = sem("p1_gate_transposed")
        s_gT = sem("p1_gT")
        s_psS = sem("p1_shared")
        s_acc = sem("p1_accumulated")
        s_st = [sem(f"p1_partial_stored{r}") for r in range(R)]
        s_scat = [sem(f"p1_rows_scattered{r}") for r in range(R)]
        s_z = sem("p1_zero_tile")
        s_zst = sem("p1_spare_rows_zeroed")
        s_tail = sem("p1_tail_places")
        s_tst = sem("p1_tails_zeroed")
        s_tab = sem("p1_table_steps")

        NCONST = 14
        GSTEPS = 8
        block = ctx.enter_context(nc.Block())

        @block.sync
        def _(sp):
            def load(p, c):
                i = R * p + c
                if not isinstance(i, int) or i >= R:
                    wait_apart(sp, s_r0, i - R + 1, s_passed)
                sp.dma_start(X[:, c % R, :], t["x"][bass.ts(i, P), :]).then_inc(s_x[c % R], 16)

            def store(p, c):
                i = R * p + c
                wait_apart(sp, s_acc, i + 1, s_passed)
                sp.dma_start(partial[bass.ts(i, P), :], acc[:, c % R, :]).then_inc(s_st[c % R], 16)

            load(0, 0)
            for dst, src in ((CT[:], t["cT"]), (normw[:], t["normw"]), (bin_[:], t["b_in"]),
                             (convw[:], t["conv_w"]), (convb[:], t["conv_b"]), (ebias[:], t["ebias"]),
                             (BR[1:NE + 1, :], t["br"]), (brow[:, 0:NSH, :], t["bs"]),
                             (brow[:, NSH, :], t["b_out"]), (ident[:], t["ident"]), (iota[:], t["iota"]),
                             (before[:], t["before"]), (down[:], t["down"]), (nxt[:, 0, :], t["region"])):
                sp.dma_start(dst, src).then_inc(s_const, 16)
            for dst, src in ((WIN[:], t["win"]), (WSraw[:], t["ws"]), (keep[:], t["keep"]), (tileno[:], t["tileno"])):
                sp.dma_start(dst, src).then_inc(s_w, 16)
            load(0, 1)
            load(0, 2)
            load(0, 3)
            sp.wait_ge(s_z, 1)
            for n in range(NE):
                sp.dma_start(rows[NE * REG + n * P:NE * REG + (n + 1) * P, :], zero[:]).then_inc(s_zst, 16)
            with sp.Fori(0, NT // R - 1) as p:
                for c in range(R):
                    load(p, c + R)
                    store(p, c)
            for c in range(R):
                store(NT // R - 1, c)
            for r in range(R):
                sp.wait_ge(s_st[r], 16 * (NT // R))
            sp.wait_ge(s_zst, 16 * NE)

        @block.gpsimd
        def _(pool):
            nc.gpsimd.memset(zero[:], 0.0).then_inc(s_z, 1)
            nc.gpsimd.memset(epsln[:], 1e-5)
            nc.gpsimd.memset(epsrms[:], 1e-6)
            nc.gpsimd.memset(mhalf[:], -0.5).then_inc(s_pool, 1)
            pool.wait_ge(s_pool, 1)

            def stats(p, c):
                i, q = R * p + c, c % R
                pool.wait_ge(s_mv, i + 1)
                if not isinstance(i, int) or i >= R:
                    pool.wait_ge(s_h, i - R + 1)
                nc.gpsimd.tensor_tensor(veps[:, q:q + 1], mv[:, q, 1:2], epsln[:], ALU.add).then_inc(s_pool, 1)
                pool.wait_ge(s_pool, 4 * i + 2)
                nc.gpsimd.tensor_tensor(rstd[:, q:q + 1], veps[:, q:q + 1], mhalf[:], ALU.pow).then_inc(s_rstd, 1)
                pool.wait_ge(s_rstd, i + 1)
                nc.gpsimd.tensor_tensor(msq[:, q:q + 1], rstd[:, q:q + 1], rstd[:, q:q + 1], ALU.mult).then_inc(s_pool, 1)
                pool.wait_ge(s_pool, 4 * i + 3)
                nc.gpsimd.tensor_tensor(msqe[:, q:q + 1], msq[:, q:q + 1], mv[:, q, 1:2], ALU.mult).then_inc(s_pool, 1)
                pool.wait_ge(s_pool, 4 * i + 4)
                nc.gpsimd.tensor_tensor(veps[:, q:q + 1], msqe[:, q:q + 1], epsrms[:], ALU.add).then_inc(s_pool, 1)
                pool.wait_ge(s_pool, 4 * i + 5)
                nc.gpsimd.tensor_tensor(rrms[:, q:q + 1], veps[:, q:q + 1], mhalf[:], ALU.pow).then_inc(s_rrms, 1)

            def scatter(p, c):
                i, r = R * p + c, c % R
                wait_apart(pool, s_pos, i + 1, s_passed)
                for k in range(TOPK):
                    nc.gpsimd.indirect_dma_start(
                        out=rows[:, :], out_offset=bass.IndirectOffsetOnAxis(ap=posu[:, r, k:k + 1], axis=0),
                        in_=XN[:, r, :], in_offset=None).then_inc(s_scat[r], 16)

            for c in range(3):
                stats(0, c)
            for c in range(1, R + 1):
                stats(0, c + 2)
                scatter(0, c - 1)
            with pool.Fori(1, NT // R - 1) as p:
                for c in range(1, R + 1):
                    stats(p, c + 2)
                    scatter(p, c - 1)
            for c in range(1, R):
                if c < R - 2:
                    stats(NT // R - 1, c + 2)
                scatter(NT // R - 1, c - 1)
            scatter(NT // R - 1, R - 1)
            pool.wait_ge(s_tail, 1)
            for e in range(NE):
                nc.gpsimd.indirect_dma_start(
                    out=rows[:, :], out_offset=bass.IndirectOffsetOnAxis(ap=tailu[:, e, :], axis=0),
                    in_=zero[:], in_offset=None).then_inc(s_tst, 16)
            for r in range(R):
                pool.wait_ge(s_scat[r], 32 * (NT // R))
            pool.wait_ge(s_tst, 16 * NE)

        @block.scalar
        def _(act):
            act.wait_ge(s_const, 16 * NCONST)

            def turned(p, c):
                i, q = R * p + c, c % 2
                act.wait_ge(s_psX, i + 1)
                nc.scalar.activation(XT[:, q, :, :], psX[:], ACT.Copy).then_inc(s_XT, 1)

            def experts_in(p, c):
                i = R * p + c
                act.wait_ge(s_gTps, i + 1)
                nc.scalar.activation(gT[:], psT[0:NE + 1, 0:P], ACT.Copy).then_inc(s_gT, 1)

            def normed(p, c):
                i, q, r = R * p + c, c % 2, c % R
                act.wait_ge(s_xn, i + 1)
                act.wait_ge(s_rrms, i + 1)
                if not isinstance(i, int) or i >= 2:
                    act.wait_ge(s_psX, i - 1)
                nc.scalar.activation(HN[:, q, :], XN[:, r, :], ACT.Copy, scale=rrms[:, r:r + 1]).then_inc(s_h, 1)

            def step(p, c, first=False, last=False):
                i, q = R * p + c, c % 2
                if not last:
                    normed(p, c + 1)
                if not first:
                    experts_in(p, c - 1)
                act.wait_ge(s_scm, i + 1)
                nc.scalar.activation(ex[:], scm[:], ACT.Exp, accum_out=esum[:]).then_inc(s_ex, 1)
                act.wait_ge(s_psU, i + 1)
                if not isinstance(i, int) or i >= 2:
                    act.wait_ge(s_psV, i - 1)
                for j in range(KI):
                    op = nc.scalar.activation(uT[:, q, j, HALO:HALO + P], psU[:, j, :], ACT.Identity,
                                              bias=bin_[:, j:j + 1])
                op.then_inc(s_u, 1)
                if not last:
                    act.wait_ge(s_u, i + 1)
                    if not first:
                        act.wait_ge(s_psV, i)
                    nc.scalar.activation(uT[:, 1 - q, :, 0:HALO], uT[:, q, :, P:P + HALO], ACT.Copy,
                                         scale=keep[:, at(i + 1)]).then_inc(s_halo, 1)
                    turned(p, c + 1)

            act.wait_ge(s_w, 16 * 4)
            normed(0, 0)
            turned(0, 0)
            step(0, 0, first=True)
            for c in range(1, R + 1):
                step(0, c)
            with act.Fori(1, NT // R - 1) as p:
                for c in range(1, R + 1):
                    step(p, c)
            for c in range(1, R):
                step(NT // R - 1, c, last=c == R - 1)
            experts_in(NT // R - 1, R - 1)

        @block.tensor
        def _(pe):
            pe.wait_ge(s_const, 16 * NCONST)
            pe.wait_ge(s_prep, 1)

            def transposes(p, c):
                i, q, r = R * p + c, c % 2, c % R
                pe.wait_ge(s_h, i + 1)
                if not isinstance(i, int) or i >= 1:
                    pe.wait_ge(s_XT, i)
                for j in range(2 * KD):
                    src = XN[:, r, :] if j < KD else HN[:, q, :]
                    last = nc.tensor.transpose(psX[:, j, :], src[:, (j % KD) * P:(j % KD + 1) * P], ident[:])
                last.then_inc(s_psX, 1)

            def scores(p, c):
                i, q = R * p + c, c % 2
                pe.wait_ge(s_XT, i + 1)
                if not isinstance(i, int) or i >= 1:
                    pe.wait_ge(s_gate, i)
                for k in range(KD):
                    last = nc.tensor.matmul(psG[:, 0:NE], XT[:, q, k, :], CT[:, k, :],
                                            start=(k == 0), stop=(k == KD - 1))
                last.then_inc(s_psG, 1)
            def project(p, c):
                i, q = R * p + c, c % 2
                if not isinstance(i, int) or i >= 1:
                    pe.wait_ge(s_u, i)
                for j in range(KI):
                    for k in range(KD):
                        last = nc.tensor.matmul(psU[:, j, :], WIN[:, k, j * P:(j + 1) * P], XT[:, q, KD + k, :],
                                                start=(k == 0), stop=(k == KD - 1))
                last.then_inc(s_psU, 1)

            def convolve(p, c):
                i, q = R * p + c, c % 2
                pe.wait_ge(s_u, i + 1)
                pe.wait_ge(s_halo, i + 1)
                if not isinstance(i, int) or i >= 1:
                    pe.wait_ge(s_U, i)
                for j in range(KI):
                    for k in range(TAPS):
                        last = nc.tensor.matmul(psV[:, j, :], uT[:, q, j, k:k + P], taps[:, j, k, :],
                                                start=(k == 0), stop=(k == TAPS - 1))
                last.then_inc(s_psV, 1)

            def routed(p, c):
                i, q = R * p + c, c % 2
                pe.wait_ge(s_gate, i + 1)
                if not isinstance(i, int) or i >= 1:
                    pe.wait_ge(s_place, 2 * i)
                nc.tensor.matmul(psK[:, 0:NE], before16[:], mask[:, q, :], start=True, stop=True)
                nc.tensor.matmul(psK[:, NE:2 * NE], ones[:], mask[:, q, :], start=True, stop=True).then_inc(s_rank, 1)
                if not isinstance(i, int) or i >= 1:
                    pe.wait_ge(s_gT, i)
                nc.tensor.transpose(psT[0:NE + 1, 0:P], gate[:, q, :], ident[:]).then_inc(s_gTps, 1)

            def shared(p, c):
                i, q = R * p + c, c % 2
                if not isinstance(i, int) or i >= 1:
                    pe.wait_ge(s_acc, i)
                for k in range(KD):
                    nc.tensor.matmul(psS[:, 0:D], XT[:, q, k, :], WS[:, k, :], start=(k == 0), stop=False)

            def biases(p, c):
                pe.wait_ge(s_gT, R * p + c + 1)
                nc.tensor.matmul(psS[:, 0:D], gT[:], BR[:], start=False, stop=True).then_inc(s_psS, 1)

            def step(p, c, first=False, last=False):
                scores(p, c)
                if not first:
                    routed(p, c - 1)
                project(p, c)
                if not first:
                    shared(p, c - 1)
                    biases(p, c - 1)
                if not last:
                    transposes(p, c + 1)
                convolve(p, c)

            transposes(0, 0)
            step(0, 0, first=True)
            for c in range(1, R + 1):
                step(0, c)
            with pe.Fori(1, NT // R - 1) as p:
                for c in range(1, R + 1):
                    step(p, c)
            for c in range(1, R):
                step(NT // R - 1, c, last=c == R - 1)
            routed(NT // R - 1, R - 1)
            shared(NT // R - 1, R - 1)
            biases(NT // R - 1, R - 1)

        @block.vector
        def _(dve):
            dve.wait_ge(s_const, 16 * NCONST)
            dve.wait_ge(s_w, 16 * 4)
            nc.vector.tensor_tensor(brow[:, 0, :], brow[:, 0, :], brow[:, 1, :], ALU.add).then_inc(s_gs, 1)
            for k in range(KD):
                nc.vector.tensor_scalar(WIN[:, k, :], WIN[:, k, :], normw[:, k:k + 1], None, ALU.mult)
            nc.vector.tensor_tensor(WS[:], WSraw[:, :, 0, :], WSraw[:, :, 1, :], ALU.add).then_inc(s_gs, 1)
            nc.vector.memset(uT[:, 0, :, 0:HALO], 0.0).then_inc(s_halo, 1)
            nc.vector.memset(ones[:], 1.0)
            nc.vector.tensor_copy(before16[:], before[:])
            dve.wait_ge(s_gs, 2)
            nc.vector.tensor_scalar(WS[:], WS[:], 1.0 / NSH, None, ALU.mult)
            nc.vector.scalar_tensor_tensor(BR[0:1, :], brow[:, 0, :], 1.0 / NSH, brow[:, NSH, :],
                                           ALU.mult, ALU.add)
            nc.vector.tensor_tensor(taps[:], ident[:].unsqueeze(1).unsqueeze(1).to_broadcast([P, KI, TAPS, P]),
                                    convw[:].unsqueeze(3).to_broadcast([P, KI, TAPS, P]), ALU.mult)
            nc.vector.memset(gate[:, :, 0:1], 1.0).then_inc(s_prep, 1)

            def bn_stats(p, c):
                n = p + c // R
                dve.wait_ge(s_x[c % R], 16 * (n + 1))
                nc.vector.bn_stats(bn[:, c % R, :], X[:, c % R, :]).then_inc(s_bn, 1)

            def mean_var(p, c):
                wait_apart(dve, s_bn, R * p + c + 1, s_passed)
                nc.vector.bn_aggr(mv[:, c % R, :], bn[:, c % R, :]).then_inc(s_mv, 1)

            def apply(p, c):
                i, r = R * p + c, c % R
                dve.wait_ge(s_rstd, i + 1)
                n = p + c // R
                if not isinstance(n, int) or n > 0:
                    dve.wait_ge(s_scat[r], 32 * n)
                nc.vector.tensor_scalar(XN[:, r, :], X[:, r, :], mv[:, r, 0:1], rstd[:, r:r + 1],
                                        ALU.subtract, ALU.mult).then_inc(s_xn, 1)

            def residual(p, c):
                i, r = R * p + c, c % R
                n = p + c // R
                dve.wait_ge(s_xn, i + 1)
                if not isinstance(n, int) or n > 0:
                    dve.wait_ge(s_st[r], 16 * n)
                nc.vector.scalar_tensor_tensor(acc[:, r, :], XN[:, r, :], 2.0, X[:, r, :],
                                               ALU.mult, ALU.add).then_inc(s_r0, 1)

            def convolved(p, c):
                i = R * p + c
                dve.wait_ge(s_psV, i + 1)
                nc.vector.tensor_tensor(U[:, at(i), :].rearrange("p a d -> p (a d)"), psV[:].rearrange("p a b -> p (a b)"),
                                        convb[:], ALU.add).then_inc(s_U, 1)

            def summed(p, c):
                i, r = R * p + c, c % R
                dve.wait_ge(s_psS, i + 1)
                nc.vector.tensor_tensor(acc[:, r, :], psS[:, 0:D], acc[:, r, :], ALU.add).then_inc(s_acc, 1)

            def places(p, c, part):
                i, q, r = R * p + c, c % 2, c % R
                if part == 0:
                    dve.wait_ge(s_rank, i + 1)
                    if not isinstance(i, int) or i >= 1:
                        dve.wait_ge(s_place, 2 * i)
                    nc.vector.tensor_tensor(place[:, q, :], psK[:, 0:NE], nxt[:, q, :], ALU.add).then_inc(s_place, 1)
                    nc.vector.tensor_tensor(nxt[:, 1 - q, :], psK[:, NE:2 * NE], nxt[:, q, :], ALU.add).then_inc(s_place, 1)
                if part == 1:
                    dve.wait_ge(s_place, 2 * i + 1)
                    for k in range(TOPK):
                        last = nc.vector.scalar_tensor_tensor(spare_out[:, k, :], iota[:], idxf[:, q, k:k + 1], place[:, q, :],
                                                              ALU.is_equal, ALU.mult, accum_out=posf[:, q, k:k + 1])
                    last.then_inc(s_pf, 1)
                if part == 2:
                    dve.wait_ge(s_pf, i + 1)
                    nc.vector.tensor_copy(posu[:, r, :], posf[:, q, :]).then_inc(s_pos, 1)
                    nc.vector.tensor_copy(PF[:, at(i), :], posf[:, q, :])
                    nc.vector.tensor_copy(IDX[:, at(i), :], idxf[:, q, 0:TOPK])

            def step(p, c, first=False, last=0):
                i, q = R * p + c, c % 2
                b = 2 + GSTEPS * i
                dve.wait_ge(s_psG, i + 1)
                nc.vector.tensor_tensor(sc[:], psG[:, 0:NE], ebias[:], ALU.add).then_inc(s_gs, 1)
                if last == 0:
                    bn_stats(p, c + 2)
                dve.wait_ge(s_gs, b + 1)
                nc.vector.reduce_max(smax[:], sc[:], AX.X).then_inc(s_gs, 1)
                if last == 0:
                    mean_var(p, c + 2)
                dve.wait_ge(s_gs, b + 2)
                nc.vector.tensor_scalar(scm[:], sc[:], smax[:], None, ALU.subtract).then_inc(s_scm, 1)
                if last < 2:
                    apply(p, c + 1)
                if not first:
                    convolved(p, c - 1)
                dve.wait_ge(s_ex, i + 1)
                nc.vector.reciprocal(rsum[:], esum[:]).then_inc(s_gs, 1)
                if not first:
                    places(p, c - 1, 0)
                dve.wait_ge(s_gs, b + 3)
                nc.vector.tensor_scalar(pr[:], ex[:], rsum[:], None, ALU.mult).then_inc(s_gs, 1)
                if not first:
                    places(p, c - 1, 1)
                wait_apart(dve, s_gs, b + 4, s_passed)
                nc.vector.max(top8[:], pr[:]).then_inc(s_gs, 1)
                if not first:
                    places(p, c - 1, 2)
                wait_apart(dve, s_gs, b + 5, s_passed)
                nc.vector.max_index(idx8[:], top8[:], pr[:]).then_inc(s_gs, 1)
                nc.vector.tensor_copy(TOPV[:, at(i), :], top8[:, 0:TOPK])
                if last < 2:
                    residual(p, c + 1)
                dve.wait_ge(s_gs, b + 6)
                nc.vector.tensor_copy(idxf[:, q, :], idx8[:]).then_inc(s_gs, 1)
                if not first:
                    summed(p, c - 1)
                dve.wait_ge(s_gs, b + 7)
                nc.vector.tensor_scalar(one1[:], iota[:], idxf[:, q, 0:1], None, ALU.is_equal).then_inc(s_gs, 1)
                dve.wait_ge(s_gs, b + 8)
                nc.vector.scalar_tensor_tensor(mask[:, q, :], iota[:], idxf[:, q, 1:2], one1[:], ALU.is_equal,
                                               ALU.add).then_inc(s_mask, 1)
                dve.wait_ge(s_mask, i + 1)
                nc.vector.tensor_tensor(gate[:, q, 1:NE + 1], mask[:, q, :], pr[:], ALU.mult).then_inc(s_gate, 1)

            for c in range(2):
                bn_stats(0, c)
                mean_var(0, c)
            apply(0, 0)
            residual(0, 0)
            step(0, 0, first=True)
            for c in range(1, R + 1):
                step(0, c)
            with dve.Fori(1, NT // R - 1) as p:
                for c in range(1, R + 1):
                    step(p, c)
            for c in range(1, R):
                step(NT // R - 1, c, last=max(0, c - (R - 3)))
            convolved(NT // R - 1, R - 1)
            for part in range(3):
                places(NT // R - 1, R - 1, part)
            summed(NT // R - 1, R - 1)

            dve.wait_ge(s_place, 2 * NT)
            z = NT % 2
            nc.vector.tensor_scalar(tail[:], nxt[:, z, :], down[:], None, ALU.add).then_inc(s_tab, 1)
            dve.wait_ge(s_tab, 1)
            nc.vector.tensor_copy(tailu[:, :, 0], tail[:]).then_inc(s_tail, 1)
            steps = [1]

            def done(op):
                op.then_inc(s_tab, 1)
                steps[0] += 1
                dve.wait_ge(s_tab, steps[0])

            done(nc.vector.tensor_scalar(used[:, 0, :], iota[:], -float(REG), float(P - 1), ALU.mult, ALU.add))
            done(nc.vector.tensor_tensor(used[:, 1, :], nxt[:, z, :], used[:, 0, :], ALU.add))
            done(nc.vector.tensor_copy(usedi[:, 0, :], used[:, 1, :]))
            done(nc.vector.tensor_scalar(usedi[:, 1, :], usedi[:, 0, :], 7, None, ALU.arith_shift_right))
            done(nc.vector.tensor_copy(used[:, 2, :], usedi[:, 1, :]))
            nc.vector.tensor_copy(ends[:, 0, 0:1], used[:, 2, 0:1])
            done(nc.vector.tensor_tensor(ends[:, 0, 1:NE], used[:, 2, 1:NE], used[:, 2, 0:NE - 1], ALU.add))
            a = 0
            for d in (2, 4, 8):
                nc.vector.tensor_copy(ends[:, 1 - a, 0:d], ends[:, a, 0:d])
                done(nc.vector.tensor_tensor(ends[:, 1 - a, d:NE], ends[:, a, d:NE], ends[:, a, 0:NE - d], ALU.add))
                a = 1 - a
            over_tiles = ends[0:1, a, :].unsqueeze(1).to_broadcast([1, NX, NE])
            done(nc.vector.tensor_tensor(ge[:], tileno[:].unsqueeze(2).to_broadcast([1, NX, NE]), over_tiles, ALU.is_ge))
            done(nc.vector.tensor_tensor(geb[:], ge[:], over_tiles, ALU.mult))
            nc.vector.tensor_reduce(own_[:, 0, :], ge[:], AX.X, ALU.add)
            done(nc.vector.tensor_reduce(own_[:, 1, :], geb[:], AX.X, ALU.max))
            done(nc.vector.tensor_tensor(own_[:, 2, :], tileno[:], own_[:, 1, :], ALU.subtract))
            done(nc.vector.tensor_scalar(own_[:, 2, :], own_[:, 2, :], float(P), None, ALU.mult))
            done(nc.vector.tensor_scalar(own_[:, 3, :], own_[:, 0, :], float(REG), None, ALU.mult))
            done(nc.vector.tensor_tensor(own_[:, 2, :], own_[:, 2, :], own_[:, 3, :], ALU.add))
            done(nc.vector.tensor_scalar(own_[:, 1, :], own_[:, 0, :], float(NE - 1), float(D), ALU.min, ALU.mult))
            done(nc.vector.tensor_copy(TAB[:, 0, :], own_[:, 2, :]))
            done(nc.vector.tensor_copy(TAB[:, 1, :], own_[:, 1, :]))
            done(nc.vector.tensor_tensor(shift[:, 0, :], ends[:, a, :], used[:, 2, :], ALU.subtract))
            nc.vector.tensor_scalar(shift[:, 0, :], shift[:, 0, :], float(P), None, ALU.mult)
            done(nc.vector.tensor_scalar(shift[:, 1, :], iota[:], float(REG), None, ALU.mult))
            done(nc.vector.tensor_tensor(shift[:, 0, :], shift[:, 0, :], shift[:, 1, :], ALU.subtract))
            for k in range(TOPK):
                done(nc.vector.tensor_tensor(hit, IDX[:, :, k:k + 1].to_broadcast([P, NT, NE]),
                                             iota[:].unsqueeze(1).to_broadcast([P, NT, NE]), ALU.is_equal))
                done(nc.vector.tensor_tensor(hit, hit, shift[:, 0, :].unsqueeze(1).to_broadcast([P, NT, NE]), ALU.mult))
                done(nc.vector.tensor_reduce(moved[:, 0, :, k], hit, AX.X, ALU.add))
            done(nc.vector.tensor_tensor(moved[:, 1, :, :], moved[:, 0, :, :], PF[:], ALU.add))
            done(nc.vector.tensor_copy(POS[:], moved[:, 1, :, :]))


def powers_and_experts(nc, t, route, rows, results, table, stash):
    ctx = ExitStack()
    with ctx:
        def sb(name, shape, dt=F32):
            return ctx.enter_context(nc.sbuf_tensor(name, shape, dt))

        def pb(name, shape, dt=F32):
            return ctx.enter_context(nc.psum_tensor(name, shape, dt))

        def sem(name):
            return ctx.enter_context(nc.semaphore(name))

        def sems(name, n):
            return [sem(f"{name}{k}") for k in range(n)]

        POS, TOPV, TAB = route
        NH = NB // 2
        TPB = NX // NH
        RX, RY = 6, 3
        W = sb("W", [P, KD, NE * D])
        ident = sb("identE", [P, P])
        XE = sb("XE", [P, RX, D])
        XTE = sb("XTE", [P, 2, KD, P])
        YE = sb("YE", [P, RY, D])
        psX = [pb(f"psXE{q}", [P, KD, P]) for q in range(2)]
        psY = [pb(f"psYE{q}", [P, D]) for q in range(2)]
        s_passed = sem("pe_waits_passed")
        s_c = sem("pe_const")
        s_w = sem("pe_weights")
        s_x = sems("pe_rows_loaded", RX)
        s_psX = sem("pe_transposed")
        s_XT = sem("pe_XT")
        s_psY = sem("pe_product")
        s_Y = sem("pe_copied")
        s_st = sems("pe_stored", RY)

        A1 = sb("A1", [P, NG, NST])
        A1T = sb("A1T", [P, NG, NST])
        Bv = sb("Bv", [P, NG])
        Cv = sb("Cv", [P, NG])
        own = sb("own", [P, CG])
        zero = sb("zero", [NG, (P - 1) * CG])
        Dm = [sb(f"Dm{z}", [P, GB, P]) for z in range(2)]
        DT = [sb(f"DT{z}", [P, GB, P]) for z in range(2)]
        XR = [sb(f"XR{z}", [P, GB, P + NST]) for z in range(2)]
        YR = [sb(f"YR{z}", [P, GB, P + 1 + NST]) for z in range(2)]
        Bblk = [sb(f"Bblk{z}", [P, GB, CG]) for z in range(2)]
        KT = [sb(f"KT{z}", [P, GB, CG]) for z in range(2)]
        QG = [sb(f"QG{z}", [P, GB, P]) for z in range(2)]
        psA = [pb(f"psA{z}", [P, GB, P]) for z in range(2)]
        psB = [pb(f"psB{z}", [P, GB, P]) for z in range(2)]
        s_zero = sem("pw_zero")
        s_tz = sem("pw_table_zeroed")
        s_clear = sem("pw_cleared")
        s_init = sems("pw_start", 2)
        s_initd = sems("pw_start_diagonal_t", 2)
        s_y1 = sems("pw_first_step", 2)
        s_y1c = sems("pw_first_step_copied", 2)
        s_lev = sems("pw_level", 2)
        s_xc = sems("pw_level_x_copied", 2)
        s_dt = sems("pw_level_diagonal_t", 2)
        s_yc = sems("pw_level_y_copied", 2)
        s_d = sems("pw_level_diagonal", 2)
        s_psK = sems("pw_impulse", 2)
        s_KT = sems("pw_impulse_copied", 2)
        s_qgp = sems("pw_turned", 2)
        s_QG = sems("pw_QG", 2)
        s_stp = sems("pw_powers_stored", 2)
        s_str = sems("pw_responses_stored", 2)
        NCONST = 6
        block = ctx.enter_context(nc.Block())

        def bodies(eng, body):
            body(0)
            with eng.Fori(1, NH - 1) as h:
                body(h)
            body(NH - 1)

        def width(m, more):
            return max(WIDE, m + NST + more)

        def slots(power, tile, early=lambda u: None):
            order = [("first", 0), ("first", 1)]
            order += [("level", z, n) for n in range(LEVELS) for z in range(2)]
            order += [("finish", 0), ("finish", 1)]
            for u, piece in enumerate(order):
                early(u)
                power(*piece)
                tile(u)

        assert 2 * (LEVELS + 2) == TPB and TPB % RX == 0

        @block.sync
        def _(sp):
            for dst, src in ((A1[:], t["A"]), (A1T[:], t["AT"]), (Bv[:], t["B"]), (Cv[:], t["C"]),
                             (own[:], t["own"]), (ident[:], t["ident"])):
                sp.dma_start(dst, src).then_inc(s_c, 16)

            def load(h, u):
                i = TPB * h + u
                row = sp.value_load(TAB[0:1, 0, at(i)], min_val=0, max_val=(NE + 1) * REG - P)
                if not isinstance(i, int) or i >= RX:
                    wait_apart(sp, s_psX, i - RX + 1, s_passed)
                sp.dma_start(XE[:, u % RX, :], rows[bass.ds(row, P), :]).then_inc(s_x[u % RX], 16)

            def store(h, u):
                i = TPB * h + u
                wait_apart(sp, s_Y, i + 1, s_passed)
                sp.dma_start(results[bass.ts(i, P), :], YE[:, u % RY, :]).then_inc(s_st[u % RY], 16)

            for u in range(RX - 1):
                load(0, u)
            for k in range(KD):
                for e in range(4):
                    n = NE * D // 4
                    sp.dma_start(W[:, k, e * n:(e + 1) * n], t["wr"][:, k, e * n:(e + 1) * n]).then_inc(s_w, 16)
            sp.wait_ge(s_zero, 1)
            sp.dma_start(bass.AP(table, P * CG, [[TROWS * CG, NG], [1, (P - 1) * CG]]), zero[:]).then_inc(s_tz, 16)

            def body(h):
                for u in range(TPB):
                    if not isinstance(h, int) or TPB * h + u + RX - 1 < NX:
                        load(h, u + RX - 1)
                    store(h, u)

            bodies(sp, body)
            for r in range(RY):
                sp.wait_ge(s_st[r], 16 * (NX // RY))
            sp.wait_ge(s_tz, 16)

        def spread(eng, out, compact):
            return eng.tensor_tensor(out[:].rearrange("p j (c s) -> p j c s", c=CG),
                                     compact.unsqueeze(2).to_broadcast([P, GB, CG, NST]),
                                     own[:].unsqueeze(1).unsqueeze(3).to_broadcast([P, GB, CG, NST]), ALU.mult)

        def groups(h, z):
            k = 2 * h + z
            return slice(GB * k, GB * (k + 1)) if isinstance(k, int) else bass.ds(GB * k, GB)

        @block.gpsimd
        def _(pool):
            nc.gpsimd.memset(zero[:], 0.0).then_inc(s_zero, 1)
            pool.wait_ge(s_c, 16 * NCONST)

            def body(h):
                def power(what, z, n=0):
                    if what == "first":
                        if not isinstance(h, int) or h > 0:
                            pool.wait_ge(s_lev[z], LEVELS * h)
                        spread(nc.gpsimd, DT[z], A1T[:, groups(h, z), :]).then_inc(s_initd[z], 1)
                    if what == "level" and n < LEVELS - 1:
                        pool.wait_ge(s_xc[z], LEVELS * h + n + 1)
                        spread(nc.gpsimd, DT[z], XR[z][:, :, P:P + NST]).then_inc(s_dt[z], 1)
                slots(power, lambda u: None)

            bodies(pool, body)

        @block.scalar
        def _(act):
            def body(h):
                def power(what, z, n=0):
                    if what == "level":
                        if n == LEVELS - 1 and z == 1:
                            store_powers(0)
                        m, w = 1 << n, width(1 << n, 0)
                        act.wait_ge(s_lev[z], LEVELS * h + n + 1)
                        nc.scalar.activation(XR[z][:, :, P:P + NST], psA[z][:, :, w - NST:w], ACT.Copy)
                        nc.scalar.activation(XR[z][:, :, P - 2 * m:P - m], psA[z][:, :, w - NST - m:w - NST],
                                             ACT.Copy).then_inc(s_xc[z], 1)
                    if what == "finish":
                        if z == 0:
                            store_powers(1)
                        k = 2 * h + z
                        act.wait_ge(s_psK[z], h + 1)
                        if not isinstance(h, int) or h > 0:
                            act.wait_ge(s_str[z], 32 * h)
                        nc.scalar.activation(KT[z][:], psA[z][:, :, 0:CG], ACT.Copy).then_inc(s_KT[z], 1)
                        act.wait_ge(s_qgp[z], h + 1)
                        nc.scalar.activation(QG[z][:], psB[z][:], ACT.Copy).then_inc(s_QG[z], 1)
                        wait_apart(act, s_KT[z], h + 1, s_passed)
                        act.dma_start(bass.AP(table, k * (GB * TROWS * CG), [[CG, P], [TROWS * CG, GB], [1, CG]]),
                                      KT[z][:]).then_inc(s_str[z], 16)
                        wait_apart(act, s_QG[z], h + 1, s_passed)
                        act.dma_start(stash[at(k), 2, :, :, :].rearrange("a p j c -> p (a j) c"), QG[z][:]).then_inc(s_str[z], 16)

                def store_powers(z):
                    k = 2 * h + z
                    wait_apart(act, s_d[z], LEVELS * (h + 1), s_passed)
                    for m, src in enumerate((Dm[z][:], YR[z][:, :, 0:P])):
                        act.dma_start(stash[at(k), m, :, :, :].rearrange("a p j c -> p (a j) c"), src).then_inc(s_stp[z], 16)

                def tile(u):
                    i, q = TPB * h + u, u % 2
                    act.wait_ge(s_psX, i + 1)
                    if not isinstance(i, int) or i >= 2:
                        act.wait_ge(s_psY, i - 1)
                    nc.scalar.activation(XTE[:, q, :, :], psX[q][:], ACT.Copy).then_inc(s_XT, 1)
                slots(power, lambda u: None, early=tile)

            bodies(act, body)
            for z in range(2):
                act.wait_ge(s_stp[z], 32 * NH)
                act.wait_ge(s_str[z], 32 * NH)

        @block.vector
        def _(dve):
            dve.wait_ge(s_c, 16 * NCONST)

            for z in range(2):
                nc.vector.memset(XR[z][:], 0.0).then_inc(s_clear, 1)
                nc.vector.memset(YR[z][:], 0.0).then_inc(s_clear, 1)
            dve.wait_ge(s_clear, 4)

            def start(h, z):
                g = groups(h, z)
                if not isinstance(h, int) or h > 0:
                    dve.wait_ge(s_stp[z], 32 * h)
                    dve.wait_ge(s_qgp[z], h)
                nc.vector.tensor_copy(XR[z][:, :, P - 1], Bv[:, g])
                nc.vector.tensor_copy(XR[z][:, :, P:P + NST], A1T[:, g, :])
                nc.vector.tensor_copy(YR[z][:, :, P], Cv[:, g])
                nc.vector.tensor_copy(YR[z][:, :, P + 1:P + 1 + NST], A1[:, g, :])
                nc.vector.tensor_tensor(Bblk[z][:], own[:].unsqueeze(1).to_broadcast([P, GB, CG]),
                                        Bv[:, g].unsqueeze(2).to_broadcast([P, GB, CG]), ALU.mult)
                spread(nc.vector, Dm[z], A1[:, g, :]).then_inc(s_init[z], 1)

            def first_step(h, z):
                dve.wait_ge(s_y1[z], h + 1)
                nc.vector.tensor_copy(YR[z][:, :, P - 1], psB[z][:, :, 0]).then_inc(s_y1c[z], 1)

            start(0, 0)

            def body(h):
                def power(what, z, n=0):
                    if what == "first" and z == 0:
                        start(h, 1)
                    if what == "first" and z == 1:
                        first_step(h, 0)
                    if what == "level":
                        m, w = 1 << n, width(1 << n, 1)
                        if n == 0 and z == 0:
                            first_step(h, 1)
                        dve.wait_ge(s_lev[z], LEVELS * h + n + 1)
                        nc.vector.tensor_copy(YR[z][:, :, P + 1:P + 1 + NST], psB[z][:, :, w - NST:w])
                        nc.vector.tensor_copy(YR[z][:, :, P - 2 * m:P - m],
                                              psB[z][:, :, w - NST - 1 - m:w - NST - 1]).then_inc(s_yc[z], 1)
                        spread(nc.vector, Dm[z], psB[z][:, :, w - NST:w]).then_inc(s_d[z], 1)
                    if what == "finish" and z == 1 and not (isinstance(h, int) and h == NH - 1):
                        start(h + 1, 0)

                def tile(u):
                    i, q, r = TPB * h + u, u % 2, u % RY
                    dve.wait_ge(s_psY, i + 1)
                    if not isinstance(h, int) or i >= RY:
                        dve.wait_ge(s_st[r], 16 * (TPB // RY * h + u // RY))
                    nc.vector.tensor_copy(YE[:, r, :], psY[q][:]).then_inc(s_Y, 1)
                slots(power, tile)

            bodies(dve, body)

        @block.tensor
        def _(pe):
            pe.wait_ge(s_c, 16 * NCONST)
            pe.wait_ge(s_w, 16 * 4 * KD)

            def turn(h, u):
                i, q, r = TPB * h + u, u % 2, u % RX
                pe.wait_ge(s_x[r], 16 * (TPB // RX * h + u // RX + 1))
                if not isinstance(i, int) or i >= 2:
                    pe.wait_ge(s_XT, i - 1)
                for k in range(KD):
                    last = nc.tensor.transpose(psX[q][:, k, :], XE[:, r, k * P:(k + 1) * P], ident[:])
                last.then_inc(s_psX, 1)

            def product(h, u):
                i, q = TPB * h + u, u % 2
                col = pe.value_load(TAB[0:1, 1, at(i)], min_val=0, max_val=(NE - 1) * D)
                pe.wait_ge(s_XT, i + 1)
                if not isinstance(i, int) or i >= 2:
                    pe.wait_ge(s_Y, i - 1)
                for k in range(KD):
                    last = nc.tensor.matmul(psY[q][:], XTE[:, q, k, :], W[:, k, bass.ds(col, D)],
                                            start=(k == 0), stop=(k == KD - 1))
                last.then_inc(s_psY, 1)

            def body(h):
                def power(what, z, n=0):
                    if what == "first":
                        pe.wait_ge(s_init[z], h + 1)
                        pe.wait_ge(s_initd[z], h + 1)
                        if not isinstance(h, int) or h > 0:
                            pe.wait_ge(s_KT[z], h)
                            pe.wait_ge(s_QG[z], h)
                        for j in range(GB):
                            last = nc.tensor.matmul(psB[z][:, j, 0:1], DT[z][:, j, :], YR[z][:, j, P:P + 1],
                                                    start=True, stop=True)
                        last.then_inc(s_y1[z], 1)
                    if what == "level":
                        m = 1 << n
                        if n == 0:
                            pe.wait_ge(s_y1c[z], h + 1)
                        else:
                            pe.wait_ge(s_d[z], LEVELS * h + n)
                            pe.wait_ge(s_dt[z], (LEVELS - 1) * h + n)
                        wx, wy = width(m, 0), width(m, 1)
                        for j in range(GB):
                            nc.tensor.matmul(psA[z][:, j, 0:wx], Dm[z][:, j, :], XR[z][:, j, P + NST - wx:P + NST],
                                             start=True, stop=True)
                        for j in range(GB):
                            last = nc.tensor.matmul(psB[z][:, j, 0:wy], DT[z][:, j, :],
                                                    YR[z][:, j, P + 1 + NST - wy:P + 1 + NST], start=True, stop=True)
                        last.then_inc(s_lev[z], 1)
                    if what == "finish":
                        pe.wait_ge(s_xc[z], LEVELS * (h + 1))
                        pe.wait_ge(s_d[z], LEVELS * (h + 1))
                        for j in range(GB):
                            last = nc.tensor.matmul(psA[z][:, j, 0:CG], YR[z][:, j, 1:P + 1], Bblk[z][:, j, :],
                                                    start=True, stop=True)
                        last.then_inc(s_psK[z], 1)
                        for j in range(GB):
                            last = nc.tensor.transpose(psB[z][:, j, :], XR[z][:, j, 0:P], ident[:])
                        last.then_inc(s_qgp[z], 1)

                def tile(u):
                    if not isinstance(h, int) or TPB * h + u + 1 < NX:
                        turn(h, u + 1)
                    product(h, u)
                slots(power, tile)

            turn(0, 0)
            bodies(pe, body)


def recurrence(nc, t, U, table, stash):
    ctx = ExitStack()
    with ctx:
        def sb(name, shape, dt=F32):
            return ctx.enter_context(nc.sbuf_tensor(name, shape, dt))

        def pb(name, shape, dt=F32):
            return ctx.enter_context(nc.psum_tensor(name, shape, dt))

        def sem(name):
            return ctx.enter_context(nc.semaphore(name))

        def sems(name, n):
            return [sem(f"{name}{k}") for k in range(n)]

        own = sb("ownR", [P, CG])
        ident = sb("identR", [P, P])
        D128 = sb("D128", [P, 2, GB, P])
        QG = sb("QGR", [P, 2, GB, P])
        YR = sb("YRR", [P, 2, GB, P])
        TO = sb("TO", [P, 2, GB, P, CG])
        US = sb("US", [P, 2, CB, NT])
        QD = sb("QD", [P, 2, CG, NT])
        q0 = sb("q0", [P, GB, BATCH, NCH])
        H = sb("H", [P, GB, BATCH, NCH])
        HM = sb("HM", [P, GB, CG, NT])
        psQ = [pb(f"psQ{n}", [P, CG, NT]) for n in range(2)]
        psS = pb("psSt", [P, GB, BATCH, NCH])
        psT = [pb(f"psT{n}", [P, CG, NT]) for n in range(GB)]

        s_passed = sem("re_waits_passed")
        s_c = sem("re_const")
        s_LQ = sems("re_state_matrices", 2)
        s_LY = sems("re_output_matrices", 2)
        s_TO = sems("re_toeplitz", 2)
        s_US = sem("re_US")
        s_psQ = sem("re_state_input")
        s_QD = sem("re_state_input_own")
        s_q0 = sem("re_q0")
        s_rec = sem("re_state_products")
        s_clear = sem("re_state_cleared")
        s_H = sem("re_state")
        s_HM = sem("re_state_spread")
        s_Tp = sem("re_toeplitz_products")
        s_T = sem("re_outputs")
        s_Uo = sem("re_outputs_copied")
        NSTEP = NCH - 2
        block = ctx.enter_context(nc.Block())

        def bodies(eng, body):
            body(0, 0, 2, 1)
            with eng.Fori(0, (NB - 4) // 2) as g:
                body(2 * g + 1, 1, 2, g + 1)
                body(2 * g + 2, 0, 2, g + 2)
            body(NB - 3, 1, 2, NB // 2 - 1)
            body(NB - 2, 0, 1, NB // 2)
            body(NB - 1, 1, 0, NB // 2)

        @block.sync
        def _(sp):
            sp.dma_start(own[:], t["own"]).then_inc(s_c, 16)
            sp.dma_start(ident[:], t["ident"]).then_inc(s_c, 16)

            def state_matrices(k, q):
                for m, dst in ((0, D128), (2, QG)):
                    sp.dma_start(dst[:, q, :, :], stash[at(k), m, :, :, :].rearrange("a p j c -> p (a j) c")).then_inc(s_LQ[q], 16)

            def output_matrices(k, q):
                sp.dma_start(YR[:, q, :, :], stash[at(k), 1, :, :, :].rearrange("a p j c -> p (a j) c")).then_inc(s_LY[q], 16)
                for j in range(GB):
                    sp.dma_start(TO[:, q, j, :, :], bass.AP(table, k * (GB * TROWS * CG) + j * TROWS * CG,
                                                            [[CG, P], [1, P * CG]])).then_inc(s_TO[q], 16)

            state_matrices(0, 0)
            state_matrices(1, 1)
            output_matrices(0, 0)

            def body(k, q, more, n):
                if more >= 1:
                    if not isinstance(k, int) or k > 0:
                        wait_apart(sp, s_T, GB * k, s_passed)
                    output_matrices(k + 1, 1 - q)
                if more >= 2:
                    wait_apart(sp, s_rec, NSTEP * (k + 1), s_passed)
                    state_matrices(k + 2, q)

            bodies(sp, body)

        @block.scalar
        def _(act):
            def gather(k, q, j):
                d0 = CB * k + CG * j
                src = U[:, :, d0:d0 + CG] if isinstance(k, int) else U[:, :, bass.ds(d0, CG)]
                nc.scalar.activation(US[:, q, j * CG:(j + 1) * CG, :], src.rearrange("p n d -> p d n"),
                                     ACT.Copy).then_inc(s_US, 1)

            for k in range(2):
                for j in range(GB):
                    gather(k, k, j)

            def body(k, q, more, n):
                for j in range(GB):
                    act.wait_ge(s_T, GB * k + j + 1)
                    d0 = CB * k + CG * j
                    dst = U[:, :, d0:d0 + CG] if isinstance(k, int) else U[:, :, bass.ds(d0, CG)]
                    nc.scalar.activation(dst.rearrange("p n e -> p e n"), psT[j][:], ACT.Copy).then_inc(s_Uo, 1)
                    if more >= 2:
                        gather(k + 2, q, j)

            bodies(act, body)

        @block.vector
        def _(dve):
            dve.wait_ge(s_c, 32)

            def own_input(k, j):
                wait_apart(dve, s_psQ, GB * k + j + 1, s_passed)
                if not isinstance(k, int) or k > 0 or j >= 2:
                    dve.wait_ge(s_q0, GB * k + j - 1)
                nc.vector.tensor_tensor(QD[:, j % 2, :, :], psQ[j % 2][:],
                                        own[:].unsqueeze(2).to_broadcast([P, CG, NT]), ALU.mult).then_inc(s_QD, 1)

            def summed(k, j):
                wait_apart(dve, s_QD, GB * k + j + 1, s_passed)
                if not isinstance(k, int) or k > 0:
                    wait_apart(dve, s_H, NCH * k, s_passed)
                nc.vector.tensor_reduce(q0[:, j, :, :].rearrange("p b c -> p (b c)"),
                                        QD[:, j % 2, :, :].rearrange("p e n -> p n e"), AX.X, ALU.add).then_inc(s_q0, 1)

            def start(k):
                if not isinstance(k, int) or k > 0:
                    dve.wait_ge(s_HM, GB * k)
                nc.vector.memset(H[:, :, :, 0], 0.0).then_inc(s_H, 1)
                for j in range(GB + 1):
                    if j < GB:
                        own_input(k, j)
                    if j >= 1:
                        summed(k, j - 1)
                dve.wait_ge(s_q0, GB * (k + 1))
                nc.vector.tensor_copy(H[:, :, :, 1], q0[:, :, :, 0]).then_inc(s_H, 1)

            def step(k, c):
                dve.wait_ge(s_rec, NSTEP * k + c)
                nc.vector.tensor_tensor(H[:, :, :, c + 1], psS[:, :, :, c], q0[:, :, :, c], ALU.add).then_inc(s_H, 1)

            def spread(k, j):
                dve.wait_ge(s_H, NCH * (k + 1))
                if not isinstance(k, int) or k > 0:
                    dve.wait_ge(s_T, GB * (k - 1) + j + 1)
                nc.vector.tensor_tensor(HM[:, j, :, :],
                                        H[:, j, :, :].rearrange("p b c -> p (b c)").unsqueeze(1).to_broadcast([P, CG, NT]),
                                        own[:].unsqueeze(2).to_broadcast([P, CG, NT]), ALU.mult).then_inc(s_HM, 1)

            def states(k):
                start(k)
                for c in range(1, NCH - 1):
                    step(k, c)
                for j in range(GB):
                    spread(k, j)

            nc.vector.memset(H[:], 0.0).then_inc(s_clear, 1)
            dve.wait_ge(s_clear, 1)
            states(0)

            def body(k, q, more, n):
                if more >= 1:
                    states(k + 1)

            bodies(dve, body)

        @block.tensor
        def _(pe):
            pe.wait_ge(s_c, 32)

            def state_input(k, q, j, n):
                pe.wait_ge(s_US, GB * k + j + 1)
                if j == 0:
                    pe.wait_ge(s_LQ[q], 32 * n)
                if not isinstance(k, int) or k > 0 or j >= 2:
                    pe.wait_ge(s_QD, GB * k + j - 1)
                nc.tensor.matmul(psQ[j % 2][:].rearrange("p e n -> p (e n)"), QG[:, q, j, :],
                                 US[:, q, j * CG:(j + 1) * CG, :].rearrange("p e n -> p (e n)"),
                                 start=True, stop=True).then_inc(s_psQ, 1)

            def step(k, q, c):
                pe.wait_ge(s_H, NCH * k + c + 1)
                for j in range(GB):
                    last = nc.tensor.matmul(psS[:, j, :, :].rearrange("p b c -> p (b c)"), D128[:, q, j, :],
                                            H[:, j, :, :].rearrange("p b c -> p (b c)"), start=True, stop=True)
                last.then_inc(s_rec, 1)

            def toeplitz(k, q, j, n, half):
                if half == 0:
                    if not isinstance(k, int) or k > 0:
                        pe.wait_ge(s_Uo, GB * (k - 1) + j + 1)
                    if j == 0:
                        pe.wait_ge(s_TO[q], 16 * GB * n)
                for e in range(CG // 2 * half, CG // 2 * (half + 1)):
                    nc.tensor.matmul(psT[j][:, e, :], TO[:, q, j, :, e], US[:, q, j * CG + e, :],
                                     start=(e == 0), stop=False, skip_group_check=True)

            def carried(k, q, j, n):
                pe.wait_ge(s_HM, GB * k + j + 1)
                if j == 0:
                    pe.wait_ge(s_LY[q], 16 * n)
                nc.tensor.matmul(psT[j][:].rearrange("p e n -> p (e n)"), YR[:, q, j, :],
                                 HM[:, j, :, :].rearrange("p e n -> p (e n)"),
                                 start=False, stop=True, skip_group_check=True).then_inc(s_T, 1)

            for j in range(GB):
                state_input(0, 0, j, 1)
            for c in range(1, NCH - 1):
                step(0, 0, c)

            def body(k, q, more, n):
                def ahead_input(j):
                    if more >= 1:
                        state_input(k + 1, 1 - q, j, n + q)

                def ahead_step(c):
                    if more >= 1:
                        step(k + 1, 1 - q, c)

                ahead_input(0)
                ahead_input(1)
                toeplitz(k, q, 0, n, 0)
                toeplitz(k, q, 0, n, 1)
                ahead_input(2)
                carried(k, q, 0, n)
                ahead_input(3)
                toeplitz(k, q, 1, n, 0)
                toeplitz(k, q, 1, n, 1)
                ahead_step(1)
                carried(k, q, 1, n)
                ahead_step(2)
                toeplitz(k, q, 2, n, 0)
                ahead_step(3)
                toeplitz(k, q, 2, n, 1)
                ahead_step(4)
                carried(k, q, 2, n)
                ahead_step(5)
                toeplitz(k, q, 3, n, 0)
                ahead_step(6)
                toeplitz(k, q, 3, n, 1)
                carried(k, q, 3, n)

            assert GB == 4 and NCH == 8
            bodies(pe, body)


def phase3(nc, t, U, route, partial, results, out):
    ctx = ExitStack()
    with ctx:
        def sb(name, shape, dt=F32):
            return ctx.enter_context(nc.sbuf_tensor(name, shape, dt))

        def pb(name, shape, dt=F32):
            return ctx.enter_context(nc.psum_tensor(name, shape, dt))

        def sem(name):
            return ctx.enter_context(nc.semaphore(name))

        POS, TOPV, TAB = route
        NBUF = 4
        pos = sb("pos3", [P, NBUF, TOPK], U32)
        gv = sb("gv", [P, 2, TOPK])
        G = sb("G3", [P, NBUF, TOPK, D])
        WO = sb("WO", [P, KI, D])
        ident = sb("ident3", [P, P])
        Y = sb("Y", [P, 2, DIN])
        YT = sb("YT", [P, 2, KI, P])
        R = sb("R", [P, NBUF, D])
        O = sb("O", [P, NBUF, D])
        psY = [pb(f"psY{n}", [P, KI, P]) for n in range(2)]
        psO = [pb(f"psO{n}", [P, 512]) for n in range(2)]
        s_passed = sem("p3_waits_passed")
        s_c = sem("p3_const")
        s_Y = sem("p3_y_staged")
        s_psY = sem("p3_y_transposed")
        s_YT = sem("p3_YT")
        s_psO = sem("p3_projected")
        s_O = sem("p3_summed")
        s_gv = sem("p3_gates_staged")
        s_add = sem("p3_partial_sums")
        s_pos = sem("p3_positions_staged")
        s_G = [sem(f"p3_results_gathered{n}") for n in range(NBUF)]
        s_R = [sem(f"p3_partial_loaded{n}") for n in range(NBUF)]
        s_out = [sem(f"p3_stored{n}") for n in range(NBUF)]
        block = ctx.enter_context(nc.Block())

        @block.sync
        def _(sp):
            sp.dma_start(WO[:], t["wout"]).then_inc(s_c, 16)
            sp.dma_start(ident[:], t["ident"]).then_inc(s_c, 16)
            sp.wait_ge(s_c, 32)
            for q in range(NBUF):
                sp.dma_start(R[:, q, :], partial[bass.ts(q, P), :]).then_inc(s_R[q], 16)
            with sp.Fori(1, NT // NBUF) as p:
                for q in range(NBUF):
                    i = NBUF * p + q
                    wait_apart(sp, s_O, i - NBUF + 1, s_passed)
                    sp.dma_start(R[:, q, :], partial[bass.ts(i, P), :]).then_inc(s_R[q], 16)

        @block.gpsimd
        def _(pool):
            def gather(i, r):
                if not isinstance(i, int) or i >= NBUF:
                    pool.wait_ge(s_O, i - NBUF + 1)
                nc.gpsimd.tensor_copy(pos[:, r, :], POS[:, at(i), :].rearrange("p a k -> p (a k)")).then_inc(s_pos, 1)
                wait_apart(pool, s_pos, i + 1, s_passed)
                for k in range(TOPK):
                    nc.gpsimd.indirect_dma_start(
                        out=G[:, r, k, :], out_offset=None, in_=results[:, :],
                        in_offset=bass.IndirectOffsetOnAxis(ap=pos[:, r, k:k + 1], axis=0)).then_inc(s_G[r], 16)

            for r in range(NBUF):
                gather(r, r)
            with pool.Fori(1, NT // NBUF) as p:
                for r in range(NBUF):
                    gather(NBUF * p + r, r)

        @block.tensor
        def _(pe):
            pe.wait_ge(s_c, 32)

            def turn(i, q):
                pe.wait_ge(s_Y, i + 1)
                if not isinstance(i, int) or i >= 2:
                    pe.wait_ge(s_YT, i - 1)
                for j in range(KI):
                    last = nc.tensor.transpose(psY[q][:, j, :], Y[:, q, j * P:(j + 1) * P], ident[:])
                last.then_inc(s_psY, 1)

            def project(i, q):
                pe.wait_ge(s_YT, i + 1)
                if not isinstance(i, int) or i >= 2:
                    pe.wait_ge(s_O, i - 1)
                for j in range(KI):
                    last = nc.tensor.matmul(psO[q][:, 0:D], YT[:, q, j, :], WO[:, j, :], start=(j == 0), stop=(j == KI - 1))
                last.then_inc(s_psO, 1)

            turn(0, 0)
            turn(1, 1)
            project(0, 0)
            with pe.Fori(1, NT // 2) as p:
                turn(2 * p, 0)
                project(2 * p - 1, 1)
                turn(2 * p + 1, 1)
                project(2 * p, 0)
            project(NT - 1, 1)

        @block.scalar
        def _(act):
            def copy(i, q):
                act.wait_ge(s_psY, i + 1)
                if not isinstance(i, int) or i >= 2:
                    act.wait_ge(s_psO, i - 1)
                nc.scalar.activation(YT[:, q, :, ::-1], psY[q][:], ACT.Copy).then_inc(s_YT, 1)

            def stage(i, q):
                if not isinstance(i, int) or i >= 2:
                    act.wait_ge(s_psY, i - 1)
                nc.scalar.activation(Y[:, q, :], U[:, at(i), :].rearrange("p a d -> p (a d)"), ACT.Copy).then_inc(s_Y, 1)

            def store(i, q):
                act.wait_ge(s_O, i + 1)
                act.dma_start(out[bass.ts(i, P), :], O[:, q, :]).then_inc(s_out[q], 16)

            stage(0, 0)
            stage(1, 1)
            for q in range(NBUF):
                copy(q, q % 2)
                stage(q + 2, q % 2)
            with act.Fori(1, NT // NBUF - 1) as p:
                for q in range(NBUF):
                    copy(NBUF * p + q, q % 2)
                    stage(NBUF * p + q + 2, q % 2)
                    store(NBUF * p + q - NBUF, q)
            for q in range(NBUF):
                copy(NT - NBUF + q, q % 2)
                if q < 2:
                    stage(NT - NBUF + q + 2, q)
                store(NT - 2 * NBUF + q, q)
            for q in range(NBUF):
                store(NT - NBUF + q, q)
            for q in range(NBUF):
                act.wait_ge(s_out[q], 16 * (NT // NBUF))

        @block.vector
        def _(dve):
            def add(i, q, n):
                dve.wait_ge(s_psO, i + 1)
                dve.wait_ge(s_R[q], 16 * n + 16)
                if not isinstance(n, int):
                    dve.wait_ge(s_out[q], 16 * n)
                nc.vector.tensor_copy(gv[:, q % 2, :], TOPV[:, at(i), :].rearrange("p a k -> p (a k)")).then_inc(s_gv, 1)
                nc.vector.tensor_tensor(O[:, q, :], psO[q % 2][:, 0:D], R[:, q, :], ALU.add).then_inc(s_add, 1)
                dve.wait_ge(s_G[q], 32 * n + 32)
                dve.wait_ge(s_gv, i + 1)
                for k in range(TOPK):
                    dve.wait_ge(s_add, 2 * i + k + 1)
                    nc.vector.scalar_tensor_tensor(O[:, q, :], G[:, q, k, :], gv[:, q % 2, k:k + 1], O[:, q, :],
                                                   ALU.mult, ALU.add).then_inc(s_add if k == 0 else s_O, 1)
            for q in range(NBUF):
                add(q, q, 0)
            with dve.Fori(1, NT // NBUF) as p:
                for q in range(NBUF):
                    add(NBUF * p + q, q, p)


def program(nc, t, out):
    partial = nc.dram_tensor("partial", [NTOK, D], F32, kind="Internal")
    rows = nc.dram_tensor("rows", [(NE + 1) * REG, D], F32, kind="Internal")
    results = nc.dram_tensor("results", [NX * P, D], F32, kind="Internal")
    stash = nc.dram_tensor("stash", [NB, 3, P, GB, P], F32, kind="Internal")
    table = nc.dram_tensor("responses", [NG, TROWS, CG], F32, kind="Internal")
    with nc.sbuf_tensor("U", [P, NT, DIN], F32) as U:
        with (nc.sbuf_tensor("POS", [P, NT, TOPK], U32) as POS, nc.sbuf_tensor("TOPV", [P, NT, TOPK], F32) as TOPV,
              nc.sbuf_tensor("TAB", [1, 2, NX], I32) as TAB):
            route = POS, TOPV, TAB
            phase1(nc, t, U, route, partial, rows)
            powers_and_experts(nc, t, route, rows, results, table, stash)
            recurrence(nc, t, U, table, stash)
            phase3(nc, t, U, route, partial, results, out)


def kernel(L0_attn_x, L0_attn_norm_w, L0_attn_Win, L0_attn_b_in, L0_attn_conv_w, L0_attn_conv_b, L0_attn_A,
           L0_attn_Bm, L0_attn_Cm, L0_attn_Wout, L0_attn_b_out, L0_ffn_centroids, L0_ffn_expert_biases,
           L0_ffn_Wr, L0_ffn_br, L0_ffn_Ws, L0_ffn_bs):
    import concourse.bacc as bacc
    from concourse.bass_utils import run_bass_kernel_spmd

    def a(v):
        return np.asarray(v)

    def blocks(v, k):
        v = a(v)
        return v.reshape((k, P) + v.shape[1:]).swapaxes(0, 1)

    A = a(L0_attn_A)
    arrays = {
        "x": a(L0_attn_x).reshape(NTOK, D),
        "normw": blocks(L0_attn_norm_w, KD),
        "win": blocks(L0_attn_Win, KD),
        "b_in": blocks(L0_attn_b_in, KI),
        "conv_w": blocks(a(L0_attn_conv_w)[:, 0, :], KI),
        "conv_b": np.broadcast_to(a(L0_attn_conv_b)[None, :], (P, DIN)),
        "A": A.reshape(NG, P, NST).transpose(1, 0, 2),
        "AT": A.transpose(0, 2, 1).reshape(NG, P, NST).transpose(1, 0, 2),
        "B": a(L0_attn_Bm).reshape(NG, P).T,
        "C": a(L0_attn_Cm).reshape(NG, P).T,
        "wout": blocks(L0_attn_Wout, KI),
        "b_out": a(L0_attn_b_out).reshape(1, D),
        "cT": blocks(a(L0_ffn_centroids).T, KD),
        "ebias": np.broadcast_to(a(L0_ffn_expert_biases)[None, :], (P, NE)),
        "wr": blocks(a(L0_ffn_Wr).transpose(2, 0, 1).reshape(D, NE * D), KD),
        "br": a(L0_ffn_br),
        "ws": blocks(a(L0_ffn_Ws).transpose(2, 0, 1), KD),
        "bs": a(L0_ffn_bs).reshape(1, NSH, D),
        "ident": np.eye(P, dtype=np.float32),
        "iota": np.tile(np.arange(NE, dtype=np.float32), (P, 1)),
        "before": np.triu(np.ones((P, P), np.float32), 1),
        "down": np.arange(P, dtype=np.float32)[:, None],
        "region": np.tile(np.arange(NE, dtype=np.float32) * REG, (P, 1)),
        "tileno": np.arange(NX, dtype=np.float32)[None, :],
        "keep": np.tile((np.arange(NT) % NCH != 0).astype(np.float32), (P, 1)),
        "own": (np.arange(P)[:, None] // NST == np.arange(CG)[None, :]).astype(np.float32),
    }
    nc = bacc.Bacc("TRN2", target_bir_lowering=False, num_devices=1)
    arrays = {f"in_{n}": np.ascontiguousarray(v) for n, v in arrays.items()}
    t = {n[3:]: nc.dram_tensor(n, v.shape, F32, kind="ExternalInput").ap() for n, v in arrays.items()}
    out = nc.dram_tensor("out_0", (NTOK, D), F32, kind="ExternalOutput").ap()
    program(nc, t, out)
    r = run_bass_kernel_spmd(nc, [arrays], core_ids=[0])
    return r.results[0]["out_0"].reshape(BATCH, SEQ, D)
```

```python
import numpy as np
import concourse.bass as bass
from concourse import mybir
from contextlib import ExitStack

F32 = mybir.dt.float32
BF16 = mybir.dt.bfloat16
U32 = mybir.dt.uint32
I32 = mybir.dt.int32
ALU = mybir.AluOpType
ACT = mybir.ActivationFunctionType
AX = mybir.AxisListType

P = 128
BATCH, SEQ, D = 8, 1024, 256
DIN, NST, TAPS = 512, 16, 4
NE, NSH, TOPK = 16, 2, 2
NTOK = BATCH * SEQ
NT = NTOK // P
NCH = SEQ // P
KD = D // P
KI = DIN // P
CG = P // NST
NG = DIN // CG
GB = 4
NB = NG // GB
CB = CG * GB
HALO = TAPS - 1
PTAPS = 1
VTAPS = TAPS - 1 - PTAPS
NX = TOPK * NT + NE
REG = NTOK + P
LEVELS = 7
WIDE = 64
TROWS = 2 * P - 1


def at(i):
    return slice(i, i + 1) if isinstance(i, int) else bass.ds(i, 1)


def wait_apart(eng, sem, value, passed):
    eng.wait_ge(sem, value)
    eng.sem_inc(passed, 1)


def phase1(nc, t, U, route, partial, rows):
    ctx = ExitStack()
    with ctx:
        def sb(name, shape, dt=F32):
            return ctx.enter_context(nc.sbuf_tensor(name, shape, dt))

        def pb(name, shape, dt=F32):
            return ctx.enter_context(nc.psum_tensor(name, shape, dt))

        def sem(name):
            return ctx.enter_context(nc.semaphore(name))

        TOPV, TAB, IDX, PF, shift = route[1:]
        R = 4
        WS = sb("WS", [P, KD, D])
        WSraw = sb("WSraw", [P, KD, NSH, D])
        WIN = sb("WIN", [P, KD, DIN])
        CT = sb("CT", [P, KD, NE])
        normw = sb("normw", [P, KD])
        bin_ = sb("bin_", [P, KI])
        convw = sb("convw", [P, KI, TAPS])
        convb = sb("convb", [P, KI])
        taps = sb("taps", [P, KI, PTAPS, P])
        ebias = sb("ebias", [P, NE])
        BR = sb("BR", [NE + 1, D])
        brow = sb("brow", [1, NSH + 1, D])
        ident = sb("ident", [P, P])
        before = sb("before", [P, P])
        ones = sb("ones", [P, P], BF16)
        iota = sb("iota", [P, NE])
        down = sb("down", [P, 1])
        keep = sb("keep", [P, NT])
        tileno = sb("tileno", [NE, NX])
        mhalf = sb("mhalf", [P, 1])
        epsln = sb("epsln", [P, 1])
        epsrms = sb("epsrms", [P, 1])
        zero = sb("zero1", [P, D])
        X = sb("X", [P, R, D])
        bn = sb("bn", [P, R, 6])
        mv = sb("mv", [P, R, 2])
        veps = sb("veps", [P, R])
        rstd = sb("rstd", [P, R])
        msq = sb("msq", [P, R])
        msqe = sb("msqe", [P, R])
        rrms = sb("rrms", [P, R])
        XN = sb("XN", [P, R, D])
        HN = sb("HN", [P, 2, D])
        XT = sb("XT", [P, 2, 2 * KD, P])
        acc = sb("acc", [P, R, D])
        uT = sb("uT", [P, 2, KI, HALO + P])
        vT = sb("vT", [P, 2, KI, P])
        sc = sb("sc", [P, NE])
        scm = sb("scm", [P, NE])
        smax = sb("smax", [P, 1])
        ex = sb("ex", [P, NE])
        esum = sb("esum", [P, 1])
        rsum = sb("rsum", [P, 1])
        pr = sb("pr", [P, NE])
        top8 = sb("top8", [P, 8])
        idx8 = sb("idx8", [P, 8], U32)
        idxf = sb("idxf", [P, 2, 8])
        one1 = sb("one1", [P, NE])
        mask = sb("mask", [P, 2, NE], BF16)
        before16 = sb("before16", [P, P], BF16)
        gate = sb("gate", [P, 2, NE + 1])
        gT = sb("gT", [NE + 1, P])
        nxt = sb("nxt", [P, 2, NE])
        place = sb("place", [P, 2, NE])
        spare_out = sb("spare_out", [P, 2, NE])
        posf = sb("posf", [P, 2, TOPK])
        posu = sb("posu", [P, R, TOPK], U32)
        taili = sb("taili", [1, NE], I32)
        used = sb("used", [P, 3, NE])
        usedi = sb("usedi", [P, 2, NE], I32)
        ends = sb("ends", [P, 2, NE])
        shift2 = sb("shift2", [P, 2, NE])
        column = sb("column", [P, 2])
        ended = sb("ended", [NE, 2, NX], BF16)
        own_ = sb("own_", [1, 4, NX])

        psX = pb("psX", [P, 2 * KD, P])
        psU = pb("psU", [P, KI, P])
        psV = pb("psV", [P, KI, P])
        psG = pb("psG", [P, 512])
        psK = pb("psRank", [P, 512])
        psT = pb("psGT", [P, 512])
        psS = pb("psS", [P, 512])

        s_passed = sem("p1_waits_passed")
        s_const = sem("p1_const_loaded")
        s_w = sem("p1_weights_loaded")
        s_prep = sem("p1_weights_prepared")
        s_x = [sem(f"p1_x_loaded{r}") for r in range(R)]
        s_bn = sem("p1_bn_stats")
        s_mv = sem("p1_mean_var")
        s_pool = sem("p1_pool_steps")
        s_rstd = sem("p1_rstd")
        s_rrms = sem("p1_rrms")
        s_xn = sem("p1_xn")
        s_h = sem("p1_h")
        s_r0 = sem("p1_residual")
        s_xxn = sem("p1_x_and_xn")
        s_psX = sem("p1_transposed")
        s_XT = sem("p1_XT")
        s_psU = sem("p1_projected")
        s_u = sem("p1_u")
        s_halo = sem("p1_halo")
        s_tap0 = sem("p1_first_tap")
        s_tap1 = sem("p1_vector_taps")
        s_psV = sem("p1_convolved")
        s_U = sem("p1_U_written")
        s_psG = sem("p1_scores")
        s_gs = sem("p1_gate_steps")
        s_scm = sem("p1_scores_shifted")
        s_ex = sem("p1_exp")
        s_gate = sem("p1_gate")
        s_rank = sem("p1_ranks")
        s_place = sem("p1_places")
        s_mask = sem("p1_mask")
        s_pf = sem("p1_positions_summed")
        s_pos = sem("p1_positions")
        s_gTps = sem("p1_gate_transposed")
        s_gT = sem("p1_gT")
        s_psS = sem("p1_shared")
        s_acc = sem("p1_accumulated")
        s_st = [sem(f"p1_partial_stored{r}") for r in range(R)]
        s_scat = [sem(f"p1_rows_scattered{r}") for r in range(R)]
        s_z = sem("p1_zero_tile")
        s_zst = sem("p1_spare_rows_zeroed")
        s_tail = sem("p1_tail_places")
        s_tst = sem("p1_tails_zeroed")
        s_tab = sem("p1_table_steps")
        s_ended = sem("p1_ended_experts")
        s_sums = sem("p1_ended_summed")

        NCONST = 14

        def zero_tails(eng, first):
            eng.wait_ge(s_tail, 1)
            for e in range(first, NE, 2):
                row = eng.value_load(taili[0:1, at(e)], min_val=0, max_val=NE * REG - P)
                eng.dma_start(rows[bass.ds(row, P), :], zero[:]).then_inc(s_tst, 16)

        GSTEPS = 8
        block = ctx.enter_context(nc.Block())

        @block.sync
        def _(sp):
            def load(p, c):
                i = R * p + c
                if not isinstance(i, int) or i >= R:
                    wait_apart(sp, s_r0, i - R + 1, s_passed)
                sp.dma_start(X[:, c % R, :], t["x"][bass.ts(i, P), :]).then_inc(s_x[c % R], 16)

            def store(p, c):
                i = R * p + c
                wait_apart(sp, s_acc, i + 1, s_passed)
                sp.dma_start(partial[bass.ts(i, P), :], acc[:, c % R, :]).then_inc(s_st[c % R], 16)

            load(0, 0)
            load(0, 1)
            for dst, src in ((CT[:], t["cT"]), (normw[:], t["normw"]), (bin_[:], t["b_in"]),
                             (convw[:], t["conv_w"]), (convb[:], t["conv_b"]), (ebias[:], t["ebias"]),
                             (BR[1:NE + 1, :], t["br"]), (brow[:, 0:NSH, :], t["bs"]),
                             (brow[:, NSH, :], t["b_out"]), (ident[:], t["ident"]), (iota[:], t["iota"]),
                             (before[:], t["before"]), (down[:], t["down"]), (nxt[:, 0, :], t["region"])):
                sp.dma_start(dst, src).then_inc(s_const, 16)
            load(0, 2)
            load(0, 3)
            sp.wait_ge(s_z, 1)
            for n in range(NE):
                sp.dma_start(rows[NE * REG + n * P:NE * REG + (n + 1) * P, :], zero[:]).then_inc(s_zst, 16)
            with sp.Fori(0, NT // R - 1) as p:
                for c in range(R):
                    load(p, c + R)
                    store(p, c)
            for c in range(R):
                store(NT // R - 1, c)
            zero_tails(sp, 0)
            for r in range(R):
                sp.wait_ge(s_st[r], 16 * (NT // R))
            sp.wait_ge(s_zst, 16 * NE)
            sp.wait_ge(s_tst, 16 * NE)

        @block.gpsimd
        def _(pool):
            nc.gpsimd.memset(zero[:], 0.0).then_inc(s_z, 1)
            nc.gpsimd.memset(epsln[:], 1e-5)
            nc.gpsimd.memset(epsrms[:], 1e-6)
            nc.gpsimd.memset(mhalf[:], -0.5).then_inc(s_pool, 1)
            pool.wait_ge(s_pool, 1)

            def stats(p, c):
                i, q = R * p + c, c % R
                pool.wait_ge(s_mv, i + 1)
                if not isinstance(i, int) or i >= R:
                    pool.wait_ge(s_h, i - R + 1)
                nc.gpsimd.tensor_tensor(veps[:, q:q + 1], mv[:, q, 1:2], epsln[:], ALU.add).then_inc(s_pool, 1)
                pool.wait_ge(s_pool, 4 * i + 2)
                nc.gpsimd.tensor_tensor(rstd[:, q:q + 1], veps[:, q:q + 1], mhalf[:], ALU.pow).then_inc(s_rstd, 1)
                pool.wait_ge(s_rstd, i + 1)
                nc.gpsimd.tensor_tensor(msq[:, q:q + 1], rstd[:, q:q + 1], rstd[:, q:q + 1], ALU.mult).then_inc(s_pool, 1)
                pool.wait_ge(s_pool, 4 * i + 3)
                nc.gpsimd.tensor_tensor(msqe[:, q:q + 1], msq[:, q:q + 1], mv[:, q, 1:2], ALU.mult).then_inc(s_pool, 1)
                pool.wait_ge(s_pool, 4 * i + 4)
                nc.gpsimd.tensor_tensor(veps[:, q:q + 1], msqe[:, q:q + 1], epsrms[:], ALU.add).then_inc(s_pool, 1)
                pool.wait_ge(s_pool, 4 * i + 5)
                nc.gpsimd.tensor_tensor(rrms[:, q:q + 1], veps[:, q:q + 1], mhalf[:], ALU.pow).then_inc(s_rrms, 1)

            def residual(p, c):
                i, r = R * p + c, c % R
                n = p + c // R
                pool.wait_ge(s_xn, i + 1)
                if not isinstance(n, int) or n > 0:
                    pool.wait_ge(s_st[r], 16 * n)
                nc.gpsimd.tensor_tensor(acc[:, r, :], XN[:, r, :], X[:, r, :], ALU.add).then_inc(s_xxn, 1)
                pool.wait_ge(s_xxn, i + 1)
                nc.gpsimd.tensor_tensor(acc[:, r, :], acc[:, r, :], XN[:, r, :], ALU.add).then_inc(s_r0, 1)

            def scatter(p, c):
                i, r = R * p + c, c % R
                wait_apart(pool, s_pos, i + 1, s_passed)
                for k in range(TOPK):
                    nc.gpsimd.indirect_dma_start(
                        out=rows[:, :], out_offset=bass.IndirectOffsetOnAxis(ap=posu[:, r, k:k + 1], axis=0),
                        in_=XN[:, r, :], in_offset=None).then_inc(s_scat[r], 16)

            stats(0, 0)
            stats(0, 1)
            residual(0, 0)
            stats(0, 2)
            residual(0, 1)
            for c in range(1, R + 1):
                stats(0, c + 2)
                residual(0, c + 1)
                scatter(0, c - 1)
            with pool.Fori(1, NT // R - 1) as p:
                for c in range(1, R + 1):
                    stats(p, c + 2)
                    residual(p, c + 1)
                    scatter(p, c - 1)
            for c in range(1, R):
                if c < R - 2:
                    stats(NT // R - 1, c + 2)
                if c < R - 1:
                    residual(NT // R - 1, c + 1)
                scatter(NT // R - 1, c - 1)
            scatter(NT // R - 1, R - 1)
            for r in range(R):
                pool.wait_ge(s_scat[r], 32 * (NT // R))

        @block.scalar
        def _(act):
            for dst, src in ((WIN[:], t["win"]), (WSraw[:], t["ws"]), (keep[:], t["keep"]), (tileno[:], t["tileno"])):
                act.dma_start(dst, src).then_inc(s_w, 16)
            act.wait_ge(s_const, 16 * NCONST)

            def turned(p, c):
                i, q = R * p + c, c % 2
                act.wait_ge(s_psX, i + 1)
                nc.scalar.activation(XT[:, q, :, :], psX[:], ACT.Copy).then_inc(s_XT, 1)

            def experts_in(p, c):
                i = R * p + c
                act.wait_ge(s_gTps, i + 1)
                nc.scalar.activation(gT[:], psT[0:NE + 1, 0:P], ACT.Copy).then_inc(s_gT, 1)

            def convolved(p, c):
                i = R * p + c
                act.wait_ge(s_psV, i + 1)
                nc.scalar.activation(U[:, at(i), :], psV[:].rearrange("p a b -> p (a b)"), ACT.Copy).then_inc(s_U, 1)

            def normed(p, c):
                i, q, r = R * p + c, c % 2, c % R
                act.wait_ge(s_xn, i + 1)
                act.wait_ge(s_rrms, i + 1)
                if not isinstance(i, int) or i >= 2:
                    act.wait_ge(s_psX, i - 1)
                nc.scalar.activation(HN[:, q, :], XN[:, r, :], ACT.Copy, scale=rrms[:, r:r + 1]).then_inc(s_h, 1)

            def step(p, c, first=False, second=True, last=False):
                i, q = R * p + c, c % 2
                if not last:
                    normed(p, c + 1)
                if not first:
                    experts_in(p, c - 1)
                act.wait_ge(s_scm, i + 1)
                nc.scalar.activation(ex[:], scm[:], ACT.Exp, accum_out=esum[:]).then_inc(s_ex, 1)
                if not first and second:
                    convolved(p, c - 2)
                if not first:
                    act.wait_ge(s_u, i)
                    if second:
                        act.wait_ge(s_psV, i - 1)
                    nc.scalar.activation(uT[:, q, :, 0:HALO], uT[:, 1 - q, :, P:P + HALO], ACT.Copy,
                                         scale=keep[:, at(i)]).then_inc(s_halo, 1)
                act.wait_ge(s_psU, i + 1)
                if not isinstance(i, int) or i >= 2:
                    act.wait_ge(s_psV, i - 1)
                for j in range(KI):
                    op = nc.scalar.activation(uT[:, q, j, HALO:HALO + P], psU[:, j, :], ACT.Identity,
                                              bias=bin_[:, j:j + 1])
                op.then_inc(s_u, 1)
                act.wait_ge(s_u, i + 1)
                act.wait_ge(s_halo, i + 1)
                for j in range(KI):
                    op = nc.scalar.activation(vT[:, q, j, :], uT[:, q, j, 0:P], ACT.Identity,
                                              bias=convb[:, j:j + 1], scale=convw[:, j, 0:1])
                op.then_inc(s_tap0, 1)
                if not last:
                    turned(p, c + 1)

            act.wait_ge(s_w, 16 * 4)
            normed(0, 0)
            turned(0, 0)
            step(0, 0, first=True)
            for c in range(1, R + 1):
                step(0, c, second=c > 1)
            with act.Fori(1, NT // R - 1) as p:
                for c in range(1, R + 1):
                    step(p, c)
            for c in range(1, R):
                step(NT // R - 1, c, last=c == R - 1)
            convolved(NT // R - 1, R - 2)
            convolved(NT // R - 1, R - 1)
            experts_in(NT // R - 1, R - 1)
            act.wait_ge(s_z, 1)
            zero_tails(act, 1)
            act.wait_ge(s_tst, 16 * NE)

        @block.tensor
        def _(pe):
            pe.wait_ge(s_const, 16 * NCONST)
            pe.wait_ge(s_prep, 1)

            def transposes(p, c):
                i, q, r = R * p + c, c % 2, c % R
                pe.wait_ge(s_h, i + 1)
                if not isinstance(i, int) or i >= 1:
                    pe.wait_ge(s_XT, i)
                for j in range(2 * KD):
                    src = XN[:, r, :] if j < KD else HN[:, q, :]
                    last = nc.tensor.transpose(psX[:, j, :], src[:, (j % KD) * P:(j % KD + 1) * P], ident[:])
                last.then_inc(s_psX, 1)

            def scores(p, c):
                i, q = R * p + c, c % 2
                pe.wait_ge(s_XT, i + 1)
                if not isinstance(i, int) or i >= 1:
                    pe.wait_ge(s_gate, i)
                for k in range(KD):
                    last = nc.tensor.matmul(psG[:, 0:NE], XT[:, q, k, :], CT[:, k, :],
                                            start=(k == 0), stop=(k == KD - 1))
                last.then_inc(s_psG, 1)
            def project(p, c):
                i, q = R * p + c, c % 2
                if not isinstance(i, int) or i >= 1:
                    pe.wait_ge(s_u, i)
                for j in range(KI):
                    for k in range(KD):
                        last = nc.tensor.matmul(psU[:, j, :], WIN[:, k, j * P:(j + 1) * P], XT[:, q, KD + k, :],
                                                start=(k == 0), stop=(k == KD - 1))
                last.then_inc(s_psU, 1)

            def convolve(p, c):
                i, q = R * p + c, c % 2
                pe.wait_ge(s_u, i + 1)
                pe.wait_ge(s_halo, i + 1)
                if not isinstance(i, int) or i >= 1:
                    pe.wait_ge(s_U, i)
                pe.wait_ge(s_tap1, VTAPS * KI * (i + 1))
                for j in range(KI):
                    for k in range(PTAPS):
                        n = TAPS - PTAPS + k
                        nc.tensor.matmul(psV[:, j, :], uT[:, q, j, n:n + P], taps[:, j, k, :],
                                         start=(k == 0), stop=False)
                    last = nc.tensor.matmul(psV[:, j, :], vT[:, q, j, :], ident[:], start=False, stop=True)
                last.then_inc(s_psV, 1)

            def routed(p, c):
                i, q = R * p + c, c % 2
                pe.wait_ge(s_gate, i + 1)
                if not isinstance(i, int) or i >= 1:
                    pe.wait_ge(s_place, 2 * i)
                nc.tensor.matmul(psK[:, 0:NE], before16[:], mask[:, q, :], start=True, stop=True)
                nc.tensor.matmul(psK[:, NE:2 * NE], ones[:], mask[:, q, :], start=True, stop=True).then_inc(s_rank, 1)
                if not isinstance(i, int) or i >= 1:
                    pe.wait_ge(s_gT, i)
                nc.tensor.transpose(psT[0:NE + 1, 0:P], gate[:, q, :], ident[:]).then_inc(s_gTps, 1)

            def shared(p, c):
                i, q = R * p + c, c % 2
                if not isinstance(i, int) or i >= 1:
                    pe.wait_ge(s_acc, i)
                for k in range(KD):
                    nc.tensor.matmul(psS[:, 0:D], XT[:, q, k, :], WS[:, k, :], start=(k == 0), stop=False)

            def biases(p, c):
                pe.wait_ge(s_gT, R * p + c + 1)
                nc.tensor.matmul(psS[:, 0:D], gT[:], BR[:], start=False, stop=True).then_inc(s_psS, 1)

            def step(p, c, first=False, last=False):
                scores(p, c)
                if not first:
                    routed(p, c - 1)
                project(p, c)
                if not first:
                    shared(p, c - 1)
                    biases(p, c - 1)
                if not last:
                    transposes(p, c + 1)
                if not first:
                    convolve(p, c - 1)

            transposes(0, 0)
            step(0, 0, first=True)
            for c in range(1, R + 1):
                step(0, c)
            with pe.Fori(1, NT // R - 1) as p:
                for c in range(1, R + 1):
                    step(p, c)
            for c in range(1, R):
                step(NT // R - 1, c, last=c == R - 1)
            convolve(NT // R - 1, R - 1)
            routed(NT // R - 1, R - 1)
            shared(NT // R - 1, R - 1)
            biases(NT // R - 1, R - 1)
            pe.wait_ge(s_ended, 1)
            nc.tensor.matmul(psK[0:1, 0:2 * NX], ones[0:NE, 0:1], ended[:].rearrange("p a n -> p (a n)"),
                             start=True, stop=True).then_inc(s_sums, 1)

        @block.vector
        def _(dve):
            def bn_stats(p, c):
                n = p + c // R
                dve.wait_ge(s_x[c % R], 16 * (n + 1))
                nc.vector.bn_stats(bn[:, c % R, :], X[:, c % R, :]).then_inc(s_bn, 1)

            def mean_var(p, c):
                wait_apart(dve, s_bn, R * p + c + 1, s_passed)
                nc.vector.bn_aggr(mv[:, c % R, :], bn[:, c % R, :]).then_inc(s_mv, 1)

            def apply(p, c):
                i, r = R * p + c, c % R
                dve.wait_ge(s_rstd, i + 1)
                n = p + c // R
                if not isinstance(n, int) or n > 0:
                    dve.wait_ge(s_scat[r], 32 * n)
                nc.vector.tensor_scalar(XN[:, r, :], X[:, r, :], mv[:, r, 0:1], rstd[:, r:r + 1],
                                        ALU.subtract, ALU.mult).then_inc(s_xn, 1)

            def summed(p, c):
                i, r = R * p + c, c % R
                dve.wait_ge(s_psS, i + 1)
                dve.wait_ge(s_r0, i + 1)
                nc.vector.tensor_tensor(acc[:, r, :], psS[:, 0:D], acc[:, r, :], ALU.add).then_inc(s_acc, 1)

            def places(p, c, part):
                i, q, r = R * p + c, c % 2, c % R
                if part == 0:
                    dve.wait_ge(s_rank, i + 1)
                    if not isinstance(i, int) or i >= 1:
                        dve.wait_ge(s_place, 2 * i)
                    nc.vector.tensor_tensor(place[:, q, :], psK[:, 0:NE], nxt[:, q, :], ALU.add).then_inc(s_place, 1)
                    nc.vector.tensor_tensor(nxt[:, 1 - q, :], psK[:, NE:2 * NE], nxt[:, q, :], ALU.add).then_inc(s_place, 1)
                if part == 1:
                    dve.wait_ge(s_place, 2 * i + 1)
                    for k in range(TOPK):
                        last = nc.vector.scalar_tensor_tensor(spare_out[:, k, :], iota[:], idxf[:, q, k:k + 1], place[:, q, :],
                                                              ALU.is_equal, ALU.mult, accum_out=posf[:, q, k:k + 1])
                    last.then_inc(s_pf, 1)
                if part == 2:
                    dve.wait_ge(s_pf, i + 1)
                    nc.vector.tensor_copy(posu[:, r, :], posf[:, q, :]).then_inc(s_pos, 1)
                    nc.vector.tensor_copy(PF[:, at(i), :], posf[:, q, :])
                    nc.vector.tensor_copy(IDX[:, at(i), :], idxf[:, q, 0:TOPK])

            def tap(p, c, n):
                i, q, k, j = R * p + c, c % 2, n // KI + 1, n % KI
                if n >= VTAPS * KI:
                    return
                if n == 0:
                    dve.wait_ge(s_tap0, i + 1)
                if k > 1:
                    dve.wait_ge(s_tap1, VTAPS * KI * i + n - KI + 1)
                nc.vector.scalar_tensor_tensor(vT[:, q, j, :], uT[:, q, j, k:k + P], convw[:, j, k:k + 1],
                                               vT[:, q, j, :], ALU.mult, ALU.add).then_inc(s_tap1, 1)

            def step(p, c, first=False, last=0):
                i, q = R * p + c, c % 2
                b = 2 + GSTEPS * i
                if last < 2:
                    apply(p, c + 1)
                if not first:
                    for n in range(KI):
                        tap(p, c - 1, n)
                dve.wait_ge(s_psG, i + 1)
                nc.vector.tensor_tensor(sc[:], psG[:, 0:NE], ebias[:], ALU.add).then_inc(s_gs, 1)
                if last == 0:
                    bn_stats(p, c + 2)
                dve.wait_ge(s_gs, b + 1)
                nc.vector.reduce_max(smax[:], sc[:], AX.X).then_inc(s_gs, 1)
                if last == 0:
                    mean_var(p, c + 2)
                dve.wait_ge(s_gs, b + 2)
                nc.vector.tensor_scalar(scm[:], sc[:], smax[:], None, ALU.subtract).then_inc(s_scm, 1)
                if not first:
                    tap(p, c - 1, 4)
                    tap(p, c - 1, 5)
                    tap(p, c - 1, 6)
                dve.wait_ge(s_ex, i + 1)
                nc.vector.reciprocal(rsum[:], esum[:]).then_inc(s_gs, 1)
                if not first:
                    places(p, c - 1, 0)
                dve.wait_ge(s_gs, b + 3)
                nc.vector.tensor_scalar(pr[:], ex[:], rsum[:], None, ALU.mult).then_inc(s_gs, 1)
                if not first:
                    places(p, c - 1, 1)
                    tap(p, c - 1, 7)
                wait_apart(dve, s_gs, b + 4, s_passed)
                nc.vector.max(top8[:], pr[:]).then_inc(s_gs, 1)
                if not first:
                    places(p, c - 1, 2)
                wait_apart(dve, s_gs, b + 5, s_passed)
                nc.vector.max_index(idx8[:], top8[:], pr[:]).then_inc(s_gs, 1)
                nc.vector.tensor_copy(TOPV[:, at(i), :], top8[:, 0:TOPK])
                dve.wait_ge(s_gs, b + 6)
                nc.vector.tensor_copy(idxf[:, q, :], idx8[:]).then_inc(s_gs, 1)
                if not first:
                    summed(p, c - 1)
                dve.wait_ge(s_gs, b + 7)
                nc.vector.tensor_scalar(one1[:], iota[:], idxf[:, q, 0:1], None, ALU.is_equal).then_inc(s_gs, 1)
                dve.wait_ge(s_gs, b + 8)
                nc.vector.scalar_tensor_tensor(mask[:, q, :], iota[:], idxf[:, q, 1:2], one1[:], ALU.is_equal,
                                               ALU.add).then_inc(s_mask, 1)
                dve.wait_ge(s_mask, i + 1)
                nc.vector.tensor_tensor(gate[:, q, 1:NE + 1], mask[:, q, :], pr[:], ALU.mult).then_inc(s_gate, 1)

            for c in range(2):
                bn_stats(0, c)
                mean_var(0, c)
            dve.wait_ge(s_const, 16 * NCONST)
            dve.wait_ge(s_w, 16 * 4)
            nc.vector.tensor_tensor(brow[:, 0, :], brow[:, 0, :], brow[:, 1, :], ALU.add).then_inc(s_gs, 1)
            for k in range(KD):
                nc.vector.tensor_scalar(WIN[:, k, :], WIN[:, k, :], normw[:, k:k + 1], None, ALU.mult)
            nc.vector.tensor_tensor(WS[:], WSraw[:, :, 0, :], WSraw[:, :, 1, :], ALU.add).then_inc(s_gs, 1)
            nc.vector.memset(uT[:, 0, :, 0:HALO], 0.0).then_inc(s_halo, 1)
            nc.vector.memset(ones[:], 1.0)
            nc.vector.tensor_copy(before16[:], before[:])
            dve.wait_ge(s_gs, 2)
            nc.vector.tensor_scalar(WS[:], WS[:], 1.0 / NSH, None, ALU.mult)
            nc.vector.scalar_tensor_tensor(BR[0:1, :], brow[:, 0, :], 1.0 / NSH, brow[:, NSH, :],
                                           ALU.mult, ALU.add)
            nc.vector.tensor_tensor(taps[:], ident[:].unsqueeze(1).unsqueeze(1).to_broadcast([P, KI, PTAPS, P]),
                                    convw[:, :, TAPS - PTAPS:TAPS].unsqueeze(3).to_broadcast([P, KI, PTAPS, P]), ALU.mult)
            nc.vector.memset(gate[:, :, 0:1], 1.0).then_inc(s_prep, 1)
            apply(0, 0)
            step(0, 0, first=True)
            for c in range(1, R + 1):
                step(0, c)
            with dve.Fori(1, NT // R - 1) as p:
                for c in range(1, R + 1):
                    step(p, c)
            for c in range(1, R):
                step(NT // R - 1, c, last=max(0, c - (R - 3)))
            for n in range(VTAPS * KI):
                tap(NT // R - 1, R - 1, n)
            for part in range(3):
                places(NT // R - 1, R - 1, part)
            summed(NT // R - 1, R - 1)

            dve.wait_ge(s_place, 2 * NT)
            z = NT % 2
            nc.vector.tensor_copy(taili[:], nxt[0:1, z, :]).then_inc(s_tail, 1)
            steps = [0]

            def done(op):
                op.then_inc(s_tab, 1)
                steps[0] += 1
                dve.wait_ge(s_tab, steps[0])

            done(nc.vector.tensor_scalar(used[:, 0, :], iota[:], -float(REG), float(P - 1), ALU.mult, ALU.add))
            done(nc.vector.tensor_tensor(used[:, 1, :], nxt[:, z, :], used[:, 0, :], ALU.add))
            done(nc.vector.tensor_copy(usedi[:, 0, :], used[:, 1, :]))
            done(nc.vector.tensor_scalar(usedi[:, 1, :], usedi[:, 0, :], 7, None, ALU.arith_shift_right))
            done(nc.vector.tensor_copy(used[:, 2, :], usedi[:, 1, :]))
            nc.vector.tensor_copy(ends[:, 0, 0:1], used[:, 2, 0:1])
            done(nc.vector.tensor_tensor(ends[:, 0, 1:NE], used[:, 2, 1:NE], used[:, 2, 0:NE - 1], ALU.add))
            a = 0
            for d in (2, 4, 8):
                nc.vector.tensor_copy(ends[:, 1 - a, 0:d], ends[:, a, 0:d])
                done(nc.vector.tensor_tensor(ends[:, 1 - a, d:NE], ends[:, a, d:NE], ends[:, a, 0:NE - d], ALU.add))
                a = 1 - a
            nc.vector.scalar_tensor_tensor(spare_out[:, 0, :], iota[:], down[:], ends[:, a, :], ALU.is_equal, ALU.mult,
                                           accum_out=column[:, 0:1])
            done(nc.vector.scalar_tensor_tensor(spare_out[:, 1, :], iota[:], down[:], used[:, 2, :], ALU.is_equal, ALU.mult,
                                                accum_out=column[:, 1:2]))
            nc.vector.tensor_scalar(ended[:, 0, :], tileno[:], column[0:NE, 0:1], None, ALU.is_ge)
            nc.vector.tensor_scalar(ended[:, 1, :], tileno[:], column[0:NE, 0:1], column[0:NE, 1:2], ALU.is_ge,
                                    ALU.mult).then_inc(s_ended, 1)
            dve.wait_ge(s_sums, 1)
            done(nc.vector.tensor_copy(own_[:, 0:2, :].rearrange("p a n -> p (a n)"), psK[0:1, 0:2 * NX]))
            done(nc.vector.tensor_tensor(own_[:, 2, :], tileno[0:1, :], own_[:, 1, :], ALU.subtract))
            done(nc.vector.tensor_scalar(own_[:, 2, :], own_[:, 2, :], float(P), None, ALU.mult))
            done(nc.vector.tensor_scalar(own_[:, 3, :], own_[:, 0, :], float(REG), None, ALU.mult))
            done(nc.vector.tensor_tensor(own_[:, 2, :], own_[:, 2, :], own_[:, 3, :], ALU.add))
            done(nc.vector.tensor_scalar(own_[:, 1, :], own_[:, 0, :], float(NE - 1), float(D), ALU.min, ALU.mult))
            done(nc.vector.tensor_copy(TAB[:, 0, :], own_[:, 2, :]))
            done(nc.vector.tensor_copy(TAB[:, 1, :], own_[:, 1, :]))
            done(nc.vector.tensor_tensor(shift2[:, 0, :], ends[:, a, :], used[:, 2, :], ALU.subtract))
            nc.vector.tensor_scalar(shift2[:, 0, :], shift2[:, 0, :], float(P), None, ALU.mult)
            done(nc.vector.tensor_scalar(shift2[:, 1, :], iota[:], float(REG), None, ALU.mult))
            done(nc.vector.tensor_tensor(shift[:], shift2[:, 0, :], shift2[:, 1, :], ALU.subtract))


def powers_and_experts(nc, t, route, rows, results, table, stash):
    ctx = ExitStack()
    with ctx:
        def sb(name, shape, dt=F32):
            return ctx.enter_context(nc.sbuf_tensor(name, shape, dt))

        def pb(name, shape, dt=F32):
            return ctx.enter_context(nc.psum_tensor(name, shape, dt))

        def sem(name):
            return ctx.enter_context(nc.semaphore(name))

        def sems(name, n):
            return [sem(f"{name}{k}") for k in range(n)]

        POS, TOPV, TAB, IDX, PF, shift = route
        NH = NB // 2
        TPB = NX // NH
        RX, RY = 6, 3
        W = sb("W", [P, KD, NE * D])
        ident = sb("identE", [P, P])
        XE = sb("XE", [P, RX, D])
        XTE = sb("XTE", [P, 2, KD, P])
        YE = sb("YE", [P, RY, D])
        psX = [pb(f"psXE{q}", [P, KD, P]) for q in range(2)]
        psY = [pb(f"psYE{q}", [P, D]) for q in range(2)]
        s_passed = sem("pe_waits_passed")
        s_c = sem("pe_const")
        s_w = sem("pe_weights")
        s_A = sem("pe_matrices")
        s_x = sems("pe_rows_loaded", RX)
        s_psX = sem("pe_transposed")
        s_XT = sem("pe_XT")
        s_psY = sem("pe_product")
        s_Y = sem("pe_copied")
        s_st = sems("pe_stored", RY)

        A1 = sb("A1", [P, NG, NST])
        A1T = sb("A1T", [P, NG, NST])
        Bv = sb("Bv", [P, NG])
        Cv = sb("Cv", [P, NG])
        own = sb("own", [P, CG])
        zero = sb("zero", [NG, (P - 1) * CG // 2])
        iota = sb("iotaE", [P, NE])
        moved = sb("moved", [P, 2, NT, TOPK])
        Dm = [sb(f"Dm{z}", [P, GB, P]) for z in range(2)]
        DT = [sb(f"DT{z}", [P, GB, P]) for z in range(2)]
        XR = [sb(f"XR{z}", [P, GB, P + NST]) for z in range(2)]
        YR = [sb(f"YR{z}", [P, GB, P + 1 + NST]) for z in range(2)]
        Bblk = [sb(f"Bblk{z}", [P, GB, CG]) for z in range(2)]
        KT = [sb(f"KT{z}", [P, GB, CG]) for z in range(2)]
        QG = sb("QG", [P, 2, GB, P])
        hit = QG[:].rearrange("p z j c -> p (z j c)").rearrange("p (n e) -> p n e", e=NE)
        psA = [pb(f"psA{z}", [P, GB, P]) for z in range(2)]
        psB = [pb(f"psB{z}", [P, GB, P]) for z in range(2)]
        s_zero = sem("pw_zero")
        s_tz = sem("pw_table_zeroed")
        s_clear = sem("pw_cleared")
        s_where = sem("pw_positions")
        s_init = sems("pw_start", 2)
        s_initd = sems("pw_start_diagonal_t", 2)
        s_y1 = sems("pw_first_step", 2)
        s_y1c = sems("pw_first_step_copied", 2)
        s_lev = sems("pw_level", 2)
        s_xc = sems("pw_level_x_copied", 2)
        s_dt = sems("pw_level_diagonal_t", 2)
        s_d = sems("pw_level_diagonal", 2)
        s_psK = sems("pw_impulse", 2)
        s_KT = sems("pw_impulse_copied", 2)
        s_qgp = sems("pw_turned", 2)
        s_QG = sems("pw_QG", 2)
        s_stp = sems("pw_powers_stored", 2)
        s_str = sems("pw_responses_stored", 2)
        NCONST = 5
        block = ctx.enter_context(nc.Block())

        def bodies(eng, body):
            body(0)
            with eng.Fori(1, NH - 1) as h:
                body(h)
            body(NH - 1)

        def width(m, more):
            return max(WIDE, m + NST + more)

        def slots(power, tile, early=lambda u: None):
            order = [("first", 0), ("first", 1)]
            order += [("level", z, n) for n in range(LEVELS) for z in range(2)]
            order += [("finish", 0), ("finish", 1)]
            for u, piece in enumerate(order):
                early(u)
                power(*piece)
                tile(u)

        assert 2 * (LEVELS + 2) == TPB and TPB % RX == 0

        @block.sync
        def _(sp):
            for dst, src in ((Bv[:], t["B"]), (Cv[:], t["C"]), (own[:], t["own"]), (ident[:], t["ident"]),
                             (iota[:], t["iota"])):
                sp.dma_start(dst, src).then_inc(s_c, 16)
            for dst, src in ((A1[:], t["A"]), (A1T[:], t["AT"])):
                sp.dma_start(dst, src).then_inc(s_A, 16)

            def load(h, u):
                i = TPB * h + u
                row = sp.value_load(TAB[0:1, 0, at(i)], min_val=0, max_val=(NE + 1) * REG - P)
                if not isinstance(i, int) or i >= RX:
                    wait_apart(sp, s_psX, i - RX + 1, s_passed)
                sp.dma_start(XE[:, u % RX, :], rows[bass.ds(row, P), :]).then_inc(s_x[u % RX], 16)

            def store(h, u):
                i = TPB * h + u
                wait_apart(sp, s_Y, i + 1, s_passed)
                sp.dma_start(results[bass.ts(i, P), :], YE[:, u % RY, :]).then_inc(s_st[u % RY], 16)

            def store_powers(h, z):
                k = 2 * h + z
                wait_apart(sp, s_d[z], LEVELS * (h + 1), s_passed)
                for m, src in enumerate((Dm[z][:], YR[z][:, :, 0:P])):
                    sp.dma_start(stash[at(k), m, :, :, :].rearrange("a p j c -> p (a j) c"), src).then_inc(s_stp[z], 16)

            def store_responses(h, z):
                k = 2 * h + z
                wait_apart(sp, s_KT[z], h + 1, s_passed)
                sp.dma_start(bass.AP(table, k * (GB * TROWS * CG), [[CG, P], [TROWS * CG, GB], [1, CG]]),
                             KT[z][:]).then_inc(s_str[z], 16)
                wait_apart(sp, s_QG[z], h + 1, s_passed)
                sp.dma_start(stash[at(k), 2, :, :, :].rearrange("a p j c -> p (a j) c"), QG[:, z, :, :]).then_inc(s_str[z], 16)

            for u in range(RX - 1):
                load(0, u)
            sp.wait_ge(s_zero, 1)
            n = (P - 1) * CG // 2
            for half in range(2):
                sp.dma_start(bass.AP(table, P * CG + half * n, [[TROWS * CG, NG], [1, n]]), zero[:]).then_inc(s_tz, 16)

            def body(h):
                for u in range(TPB):
                    if not isinstance(h, int) or TPB * h + u + RX - 1 < NX:
                        load(h, u + RX - 1)
                    store(h, u)
                    if u == 2 * LEVELS:
                        store_powers(h, 0)
                    if u == 2 * LEVELS + 1:
                        store_powers(h, 1)
                    if u == 2 * LEVELS + 2:
                        store_responses(h, 0)
                    if u == 2 * LEVELS + 3:
                        store_responses(h, 1)

            bodies(sp, body)
            for r in range(RY):
                sp.wait_ge(s_st[r], 16 * (NX // RY))
            sp.wait_ge(s_tz, 32)
            for z in range(2):
                sp.wait_ge(s_stp[z], 32 * NH)
                sp.wait_ge(s_str[z], 32 * NH)

        def spread(eng, out, compact):
            return eng.tensor_tensor(out[:].rearrange("p j (c s) -> p j c s", c=CG),
                                     compact.unsqueeze(2).to_broadcast([P, GB, CG, NST]),
                                     own[:].unsqueeze(1).unsqueeze(3).to_broadcast([P, GB, CG, NST]), ALU.mult)

        def groups(h, z):
            k = 2 * h + z
            return slice(GB * k, GB * (k + 1)) if isinstance(k, int) else bass.ds(GB * k, GB)

        @block.gpsimd
        def _(pool):
            nc.gpsimd.memset(zero[:], 0.0).then_inc(s_zero, 1)
            pool.wait_ge(s_c, 16 * NCONST)
            pool.wait_ge(s_A, 32)

            def body(h):
                def power(what, z, n=0):
                    if what == "first":
                        if not isinstance(h, int) or h > 0:
                            pool.wait_ge(s_lev[z], LEVELS * h)
                        spread(nc.gpsimd, DT[z], A1T[:, groups(h, z), :]).then_inc(s_initd[z], 1)
                    if what == "level" and n < LEVELS - 1:
                        pool.wait_ge(s_xc[z], LEVELS * h + n + 1)
                        spread(nc.gpsimd, DT[z], XR[z][:, :, P:P + NST]).then_inc(s_dt[z], 1)
                slots(power, lambda u: None)

            bodies(pool, body)

        @block.scalar
        def _(act):
            act.wait_ge(s_c, 16 * NCONST)
            for k in range(KD):
                act.dma_start(W[:, k, :], t["wr"][:, k, :]).then_inc(s_w, 16)

            def body(h):
                def power(what, z, n=0):
                    if what == "level":
                        m, w = 1 << n, width(1 << n, 0)
                        act.wait_ge(s_lev[z], LEVELS * h + n + 1)
                        nc.scalar.activation(XR[z][:, :, P:P + NST], psA[z][:, :, w - NST:w], ACT.Copy)
                        nc.scalar.activation(XR[z][:, :, P - 2 * m:P - m], psA[z][:, :, w - NST - m:w - NST],
                                             ACT.Copy).then_inc(s_xc[z], 1)
                    if what == "finish":
                        act.wait_ge(s_psK[z], h + 1)
                        if not isinstance(h, int) or h > 0:
                            act.wait_ge(s_str[z], 32 * h)
                        nc.scalar.activation(KT[z][:], psA[z][:, :, 0:CG], ACT.Copy).then_inc(s_KT[z], 1)
                        act.wait_ge(s_qgp[z], h + 1)
                        nc.scalar.activation(QG[:, z, :, :], psB[z][:], ACT.Copy).then_inc(s_QG[z], 1)

                def tile(u):
                    i, q = TPB * h + u, u % 2
                    act.wait_ge(s_psX, i + 1)
                    if not isinstance(i, int) or i >= 2:
                        act.wait_ge(s_psY, i - 1)
                    nc.scalar.activation(XTE[:, q, :, :], psX[q][:], ACT.Copy).then_inc(s_XT, 1)
                slots(power, lambda u: None, early=tile)

            bodies(act, body)

        @block.vector
        def _(dve):
            for z in range(2):
                nc.vector.memset(XR[z][:], 0.0).then_inc(s_clear, 1)
                nc.vector.memset(YR[z][:], 0.0).then_inc(s_clear, 1)
            dve.wait_ge(s_c, 16 * NCONST)
            dve.wait_ge(s_A, 32)

            dve.wait_ge(s_clear, 4)

            def start(h, z):
                g = groups(h, z)
                if not isinstance(h, int) or h > 0:
                    dve.wait_ge(s_stp[z], 32 * h)
                    dve.wait_ge(s_qgp[z], h)
                nc.vector.tensor_copy(XR[z][:, :, P - 1], Bv[:, g])
                nc.vector.tensor_copy(XR[z][:, :, P:P + NST], A1T[:, g, :])
                nc.vector.tensor_copy(YR[z][:, :, P], Cv[:, g])
                nc.vector.tensor_copy(YR[z][:, :, P + 1:P + 1 + NST], A1[:, g, :])
                nc.vector.tensor_tensor(Bblk[z][:], own[:].unsqueeze(1).to_broadcast([P, GB, CG]),
                                        Bv[:, g].unsqueeze(2).to_broadcast([P, GB, CG]), ALU.mult)
                spread(nc.vector, Dm[z], A1[:, g, :]).then_inc(s_init[z], 1)

            def first_step(h, z):
                dve.wait_ge(s_y1[z], h + 1)
                nc.vector.tensor_copy(YR[z][:, :, P - 1], psB[z][:, :, 0]).then_inc(s_y1c[z], 1)

            start(0, 0)

            def positions(n):
                if n > 0:
                    dve.wait_ge(s_where, n)
                k = n // 3
                if n == 0 or n == 3:
                    op = nc.vector.tensor_tensor(hit, IDX[:, :, k:k + 1].to_broadcast([P, NT, NE]),
                                                 iota[:].unsqueeze(1).to_broadcast([P, NT, NE]), ALU.is_equal)
                elif n == 1 or n == 4:
                    op = nc.vector.tensor_tensor(hit, hit, shift[:].unsqueeze(1).to_broadcast([P, NT, NE]), ALU.mult)
                elif n == 2 or n == 5:
                    op = nc.vector.tensor_reduce(moved[:, 0, :, k], hit, AX.X, ALU.add)
                elif n == 6:
                    op = nc.vector.tensor_tensor(moved[:, 1, :, :], moved[:, 0, :, :], PF[:], ALU.add)
                else:
                    op = nc.vector.tensor_copy(POS[:], moved[:, 1, :, :])
                op.then_inc(s_where, 1)

            def body(h):
                def power(what, z, n=0):
                    if what == "first" and z == 0:
                        start(h, 1)
                    if what == "first" and z == 1:
                        first_step(h, 0)
                    if what == "level":
                        m, w = 1 << n, width(1 << n, 1)
                        if n == 0 and z == 0:
                            first_step(h, 1)
                        dve.wait_ge(s_lev[z], LEVELS * h + n + 1)
                        nc.vector.tensor_copy(YR[z][:, :, P + 1:P + 1 + NST], psB[z][:, :, w - NST:w])
                        nc.vector.tensor_copy(YR[z][:, :, P - 2 * m:P - m],
                                              psB[z][:, :, w - NST - 1 - m:w - NST - 1])
                        spread(nc.vector, Dm[z], psB[z][:, :, w - NST:w]).then_inc(s_d[z], 1)
                        if isinstance(h, int) and h == 0 and 2 * n + z < 8:
                            positions(2 * n + z)
                    if what == "finish" and z == 1 and not (isinstance(h, int) and h == NH - 1):
                        start(h + 1, 0)

                def tile(u):
                    i, q, r = TPB * h + u, u % 2, u % RY
                    dve.wait_ge(s_psY, i + 1)
                    if not isinstance(h, int) or i >= RY:
                        dve.wait_ge(s_st[r], 16 * (TPB // RY * h + u // RY))
                    nc.vector.tensor_copy(YE[:, r, :], psY[q][:]).then_inc(s_Y, 1)
                slots(power, tile)

            bodies(dve, body)

        @block.tensor
        def _(pe):
            pe.wait_ge(s_c, 16 * NCONST)

            def turn(h, u):
                i, q, r = TPB * h + u, u % 2, u % RX
                pe.wait_ge(s_x[r], 16 * (TPB // RX * h + u // RX + 1))
                if not isinstance(i, int) or i >= 2:
                    pe.wait_ge(s_XT, i - 1)
                for k in range(KD):
                    last = nc.tensor.transpose(psX[q][:, k, :], XE[:, r, k * P:(k + 1) * P], ident[:])
                last.then_inc(s_psX, 1)

            def product(h, u):
                i, q = TPB * h + u, u % 2
                if isinstance(i, int) and i == 0:
                    pe.wait_ge(s_w, 16 * KD)
                col = pe.value_load(TAB[0:1, 1, at(i)], min_val=0, max_val=(NE - 1) * D)
                pe.wait_ge(s_XT, i + 1)
                if not isinstance(i, int) or i >= 2:
                    pe.wait_ge(s_Y, i - 1)
                for k in range(KD):
                    last = nc.tensor.matmul(psY[q][:], XTE[:, q, k, :], W[:, k, bass.ds(col, D)],
                                            start=(k == 0), stop=(k == KD - 1))
                last.then_inc(s_psY, 1)

            def body(h):
                def power(what, z, n=0):
                    if what == "first":
                        pe.wait_ge(s_init[z], h + 1)
                        pe.wait_ge(s_initd[z], h + 1)
                        if not isinstance(h, int) or h > 0:
                            pe.wait_ge(s_KT[z], h)
                            pe.wait_ge(s_QG[z], h)
                        for j in range(GB):
                            last = nc.tensor.matmul(psB[z][:, j, 0:1], DT[z][:, j, :], YR[z][:, j, P:P + 1],
                                                    start=True, stop=True)
                        last.then_inc(s_y1[z], 1)
                    if what == "level":
                        m = 1 << n
                        if n == 0:
                            pe.wait_ge(s_y1c[z], h + 1)
                        else:
                            pe.wait_ge(s_d[z], LEVELS * h + n)
                            pe.wait_ge(s_dt[z], (LEVELS - 1) * h + n)
                        wx, wy = width(m, 0), width(m, 1)
                        for j in range(GB):
                            nc.tensor.matmul(psA[z][:, j, 0:wx], Dm[z][:, j, :], XR[z][:, j, P + NST - wx:P + NST],
                                             start=True, stop=True)
                        for j in range(GB):
                            last = nc.tensor.matmul(psB[z][:, j, 0:wy], DT[z][:, j, :],
                                                    YR[z][:, j, P + 1 + NST - wy:P + 1 + NST], start=True, stop=True)
                        last.then_inc(s_lev[z], 1)
                    if what == "finish":
                        pe.wait_ge(s_xc[z], LEVELS * (h + 1))
                        pe.wait_ge(s_d[z], LEVELS * (h + 1))
                        for j in range(GB):
                            last = nc.tensor.matmul(psA[z][:, j, 0:CG], YR[z][:, j, 1:P + 1], Bblk[z][:, j, :],
                                                    start=True, stop=True)
                        last.then_inc(s_psK[z], 1)
                        for j in range(GB):
                            last = nc.tensor.transpose(psB[z][:, j, :], XR[z][:, j, 0:P], ident[:])
                        last.then_inc(s_qgp[z], 1)

                def tile(u):
                    if not isinstance(h, int) or TPB * h + u + 1 < NX:
                        turn(h, u + 1)
                    product(h, u)
                slots(power, tile)

            turn(0, 0)
            bodies(pe, body)


def recurrence(nc, t, U, table, stash):
    ctx = ExitStack()
    with ctx:
        def sb(name, shape, dt=F32):
            return ctx.enter_context(nc.sbuf_tensor(name, shape, dt))

        def pb(name, shape, dt=F32):
            return ctx.enter_context(nc.psum_tensor(name, shape, dt))

        def sem(name):
            return ctx.enter_context(nc.semaphore(name))

        def sems(name, n):
            return [sem(f"{name}{k}") for k in range(n)]

        own = sb("ownR", [P, CG])
        ident = sb("identR", [P, P])
        D128 = sb("D128", [P, 2, GB, P])
        QG = sb("QGR", [P, 2, GB, P])
        YR = sb("YRR", [P, 2, GB, P])
        TO = sb("TO", [P, 2, GB, P, CG])
        US = sb("US", [P, 2, CB, NT])
        QD = sb("QD", [P, 2, CG, NT])
        q0 = sb("q0", [P, GB, BATCH, NCH])
        H = sb("H", [P, GB, BATCH, NCH])
        HM = sb("HM", [P, GB, CG, NT])
        psQ = [pb(f"psQ{n}", [P, CG, NT]) for n in range(2)]
        psS = pb("psSt", [P, GB, BATCH, NCH])
        psT = [pb(f"psT{n}", [P, CG, NT]) for n in range(GB)]

        s_passed = sem("re_waits_passed")
        s_c = sem("re_const")
        s_LQ = sems("re_state_matrices", 2)
        s_LY = sems("re_output_matrices", 2)
        s_TO = sems("re_toeplitz", 2)
        s_US = sem("re_US")
        s_psQ = sem("re_state_input")
        s_QD = sem("re_state_input_own")
        s_q0 = sem("re_q0")
        s_rec = sem("re_state_products")
        s_clear = sem("re_state_cleared")
        s_H = sem("re_state")
        s_HM = sem("re_state_spread")
        s_HMa = sem("re_state_spread_act")
        s_T = sem("re_outputs")
        s_Uo = sem("re_outputs_copied")
        NSTEP = NCH - 2
        block = ctx.enter_context(nc.Block())

        def bodies(eng, body):
            body(0, 0, 2, 1)
            with eng.Fori(0, (NB - 4) // 2) as g:
                body(2 * g + 1, 1, 2, g + 1)
                body(2 * g + 2, 0, 2, g + 2)
            body(NB - 3, 1, 2, NB // 2 - 1)
            body(NB - 2, 0, 1, NB // 2)
            body(NB - 1, 1, 0, NB // 2)

        @block.sync
        def _(sp):
            sp.dma_start(own[:], t["own"]).then_inc(s_c, 16)
            sp.dma_start(ident[:], t["ident"]).then_inc(s_c, 16)

            def state_matrices(k, q):
                for m, dst in ((0, D128), (2, QG)):
                    sp.dma_start(dst[:, q, :, :], stash[at(k), m, :, :, :].rearrange("a p j c -> p (a j) c")).then_inc(s_LQ[q], 16)

            def output_matrices(k, q):
                sp.dma_start(YR[:, q, :, :], stash[at(k), 1, :, :, :].rearrange("a p j c -> p (a j) c")).then_inc(s_LY[q], 16)
                for j in range(GB):
                    sp.dma_start(TO[:, q, j, :, :], bass.AP(table, k * (GB * TROWS * CG) + j * TROWS * CG,
                                                            [[CG, P], [1, P * CG]])).then_inc(s_TO[q], 16)

            state_matrices(0, 0)
            state_matrices(1, 1)
            output_matrices(0, 0)

            def body(k, q, more, n):
                if more >= 1:
                    if not isinstance(k, int) or k > 0:
                        wait_apart(sp, s_T, GB * k, s_passed)
                    output_matrices(k + 1, 1 - q)
                if more >= 2:
                    wait_apart(sp, s_rec, NSTEP * (k + 1), s_passed)
                    state_matrices(k + 2, q)

            bodies(sp, body)

        @block.scalar
        def _(act):
            def gather(k, q, j):
                d0 = CB * k + CG * j
                src = U[:, :, d0:d0 + CG] if isinstance(k, int) else U[:, :, bass.ds(d0, CG)]
                nc.scalar.activation(US[:, q, j * CG:(j + 1) * CG, :], src.rearrange("p n d -> p d n"),
                                     ACT.Copy).then_inc(s_US, 1)

            def spread(k, j):
                act.wait_ge(s_H, NCH * (k + 1))
                if not isinstance(k, int) or k > 0:
                    act.wait_ge(s_T, GB * (k - 1) + j + 1)
                for e in range(CG):
                    last = nc.scalar.activation(HM[:, j, e, :], H[:, j, :, :].rearrange("p b c -> p (b c)"), ACT.Copy,
                                                scale=own[:, e:e + 1])
                last.then_inc(s_HMa, 1)

            act.wait_ge(s_c, 32)
            for k in range(2):
                for j in range(GB):
                    gather(k, k, j)

            def body(k, q, more, n):
                for j in range(2, GB):
                    spread(k, j)
                for j in range(GB):
                    act.wait_ge(s_T, GB * k + j + 1)
                    d0 = CB * k + CG * j
                    dst = U[:, :, d0:d0 + CG] if isinstance(k, int) else U[:, :, bass.ds(d0, CG)]
                    nc.scalar.activation(dst.rearrange("p n e -> p e n"), psT[j][:], ACT.Copy).then_inc(s_Uo, 1)
                    if more >= 2:
                        gather(k + 2, q, j)

            bodies(act, body)

        @block.vector
        def _(dve):
            dve.wait_ge(s_c, 32)

            def own_input(k, j):
                wait_apart(dve, s_psQ, GB * k + j + 1, s_passed)
                if not isinstance(k, int) or k > 0 or j >= 2:
                    dve.wait_ge(s_q0, GB * k + j - 1)
                nc.vector.tensor_tensor(QD[:, j % 2, :, :], psQ[j % 2][:],
                                        own[:].unsqueeze(2).to_broadcast([P, CG, NT]), ALU.mult).then_inc(s_QD, 1)

            def summed(k, j):
                wait_apart(dve, s_QD, GB * k + j + 1, s_passed)
                if not isinstance(k, int) or k > 0:
                    wait_apart(dve, s_H, NCH * k, s_passed)
                nc.vector.tensor_reduce(q0[:, j, :, :].rearrange("p b c -> p (b c)"),
                                        QD[:, j % 2, :, :].rearrange("p e n -> p n e"), AX.X, ALU.add).then_inc(s_q0, 1)

            def start(k):
                if not isinstance(k, int) or k > 0:
                    dve.wait_ge(s_HM, 2 * k)
                    dve.wait_ge(s_HMa, 2 * k)
                nc.vector.memset(H[:, :, :, 0], 0.0).then_inc(s_H, 1)
                dve.wait_ge(s_q0, GB * (k + 1))
                nc.vector.tensor_copy(H[:, :, :, 1], q0[:, :, :, 0]).then_inc(s_H, 1)

            def step(k, c):
                dve.wait_ge(s_rec, NSTEP * k + c)
                nc.vector.tensor_tensor(H[:, :, :, c + 1], psS[:, :, :, c], q0[:, :, :, c], ALU.add).then_inc(s_H, 1)

            def spread(k, j):
                dve.wait_ge(s_H, NCH * (k + 1))
                if not isinstance(k, int) or k > 0:
                    dve.wait_ge(s_T, GB * (k - 1) + j + 1)
                nc.vector.tensor_tensor(HM[:, j, :, :],
                                        H[:, j, :, :].rearrange("p b c -> p (b c)").unsqueeze(1).to_broadcast([P, CG, NT]),
                                        own[:].unsqueeze(2).to_broadcast([P, CG, NT]), ALU.mult).then_inc(s_HM, 1)

            def states(k, spreads=True):
                own_input(k, 0)
                if spreads:
                    spread(k - 1, 1)
                own_input(k, 1)
                summed(k, 0)
                own_input(k, 2)
                summed(k, 1)
                own_input(k, 3)
                summed(k, 2)
                summed(k, 3)
                start(k)
                for c in range(1, NCH - 1):
                    step(k, c)
                spread(k, 0)

            nc.vector.memset(H[:], 0.0).then_inc(s_clear, 1)
            dve.wait_ge(s_clear, 1)
            states(0, spreads=False)

            def body(k, q, more, n):
                if more >= 1:
                    states(k + 1)
                else:
                    spread(k, 1)

            bodies(dve, body)

        @block.tensor
        def _(pe):
            pe.wait_ge(s_c, 32)

            def state_input(k, q, j, n):
                pe.wait_ge(s_US, GB * k + j + 1)
                if j == 0:
                    pe.wait_ge(s_LQ[q], 32 * n)
                if not isinstance(k, int) or k > 0 or j >= 2:
                    pe.wait_ge(s_QD, GB * k + j - 1)
                nc.tensor.matmul(psQ[j % 2][:].rearrange("p e n -> p (e n)"), QG[:, q, j, :],
                                 US[:, q, j * CG:(j + 1) * CG, :].rearrange("p e n -> p (e n)"),
                                 start=True, stop=True).then_inc(s_psQ, 1)

            def step(k, q, c):
                pe.wait_ge(s_H, NCH * k + c + 1)
                for j in range(GB):
                    last = nc.tensor.matmul(psS[:, j, :, :].rearrange("p b c -> p (b c)"), D128[:, q, j, :],
                                            H[:, j, :, :].rearrange("p b c -> p (b c)"), start=True, stop=True)
                last.then_inc(s_rec, 1)

            def toeplitz(k, q, j, n, half):
                if half == 0:
                    if not isinstance(k, int) or k > 0:
                        pe.wait_ge(s_Uo, GB * (k - 1) + j + 1)
                    if j == 0:
                        pe.wait_ge(s_TO[q], 16 * GB * n)
                for e in range(CG // 2 * half, CG // 2 * (half + 1)):
                    nc.tensor.matmul(psT[j][:, e, :], TO[:, q, j, :, e], US[:, q, j * CG + e, :],
                                     start=(e == 0), stop=False, skip_group_check=True)

            def carried(k, q, j, n):
                pe.wait_ge(s_HM if j < 2 else s_HMa, 2 * k + j % 2 + 1)
                if j == 0:
                    pe.wait_ge(s_LY[q], 16 * n)
                nc.tensor.matmul(psT[j][:].rearrange("p e n -> p (e n)"), YR[:, q, j, :],
                                 HM[:, j, :, :].rearrange("p e n -> p (e n)"),
                                 start=False, stop=True, skip_group_check=True).then_inc(s_T, 1)

            for j in range(GB):
                state_input(0, 0, j, 1)
            for c in range(1, NCH - 1):
                step(0, 0, c)

            def body(k, q, more, n):
                def ahead_input(j):
                    if more >= 1:
                        state_input(k + 1, 1 - q, j, n + q)

                def ahead_step(c):
                    if more >= 1:
                        step(k + 1, 1 - q, c)

                ahead_input(0)
                ahead_input(1)
                toeplitz(k, q, 0, n, 0)
                toeplitz(k, q, 0, n, 1)
                ahead_input(2)
                carried(k, q, 0, n)
                ahead_input(3)
                toeplitz(k, q, 1, n, 0)
                toeplitz(k, q, 1, n, 1)
                carried(k, q, 1, n)
                ahead_step(1)
                toeplitz(k, q, 2, n, 0)
                ahead_step(2)
                toeplitz(k, q, 2, n, 1)
                ahead_step(3)
                carried(k, q, 2, n)
                ahead_step(4)
                toeplitz(k, q, 3, n, 0)
                ahead_step(5)
                toeplitz(k, q, 3, n, 1)
                ahead_step(6)
                carried(k, q, 3, n)

            assert GB == 4 and NCH == 8
            bodies(pe, body)


def phase3(nc, t, U, route, partial, results, out):
    ctx = ExitStack()
    with ctx:
        def sb(name, shape, dt=F32):
            return ctx.enter_context(nc.sbuf_tensor(name, shape, dt))

        def pb(name, shape, dt=F32):
            return ctx.enter_context(nc.psum_tensor(name, shape, dt))

        def sem(name):
            return ctx.enter_context(nc.semaphore(name))

        POS, TOPV = route[:2]
        NBUF = 4
        pos = sb("pos3", [P, NBUF, TOPK], U32)
        gv = sb("gv", [P, 2, TOPK])
        G = sb("G3", [P, NBUF, TOPK, D])
        WO = sb("WO", [P, KI, D])
        ident = sb("ident3", [P, P])
        Y = sb("Y", [P, 2, DIN])
        YT = sb("YT", [P, 2, KI, P])
        R = sb("R", [P, NBUF, D])
        O = sb("O", [P, NBUF, D])
        psY = [pb(f"psY{n}", [P, KI, P]) for n in range(2)]
        psO = [pb(f"psO{n}", [P, 512]) for n in range(2)]
        s_passed = sem("p3_waits_passed")
        s_c = sem("p3_const")
        s_Y = sem("p3_y_staged")
        s_psY = sem("p3_y_transposed")
        s_YT = sem("p3_YT")
        s_psO = sem("p3_projected")
        s_O = sem("p3_summed")
        s_gv = sem("p3_gates_staged")
        s_add = sem("p3_partial_sums")
        s_pos = sem("p3_positions_staged")
        s_G = [sem(f"p3_results_gathered{n}") for n in range(NBUF)]
        s_R = [sem(f"p3_partial_loaded{n}") for n in range(NBUF)]
        s_out = [sem(f"p3_stored{n}") for n in range(NBUF)]
        block = ctx.enter_context(nc.Block())

        @block.sync
        def _(sp):
            sp.dma_start(WO[:], t["wout"]).then_inc(s_c, 16)
            sp.dma_start(ident[:], t["ident"]).then_inc(s_c, 16)
            sp.wait_ge(s_c, 32)
            for q in range(NBUF):
                sp.dma_start(R[:, q, :], partial[bass.ts(q, P), :]).then_inc(s_R[q], 16)
            with sp.Fori(1, NT // NBUF) as p:
                for q in range(NBUF):
                    i = NBUF * p + q
                    wait_apart(sp, s_O, i - NBUF + 1, s_passed)
                    sp.dma_start(R[:, q, :], partial[bass.ts(i, P), :]).then_inc(s_R[q], 16)

        @block.gpsimd
        def _(pool):
            def gather(i, r):
                if not isinstance(i, int) or i >= NBUF:
                    pool.wait_ge(s_O, i - NBUF + 1)
                nc.gpsimd.tensor_copy(pos[:, r, :], POS[:, at(i), :].rearrange("p a k -> p (a k)")).then_inc(s_pos, 1)
                wait_apart(pool, s_pos, i + 1, s_passed)
                for k in range(TOPK):
                    nc.gpsimd.indirect_dma_start(
                        out=G[:, r, k, :], out_offset=None, in_=results[:, :],
                        in_offset=bass.IndirectOffsetOnAxis(ap=pos[:, r, k:k + 1], axis=0)).then_inc(s_G[r], 16)

            for r in range(NBUF):
                gather(r, r)
            with pool.Fori(1, NT // NBUF) as p:
                for r in range(NBUF):
                    gather(NBUF * p + r, r)

        @block.tensor
        def _(pe):
            pe.wait_ge(s_c, 32)

            def turn(i, q):
                pe.wait_ge(s_Y, i + 1)
                if not isinstance(i, int) or i >= 2:
                    pe.wait_ge(s_YT, i - 1)
                for j in range(KI):
                    last = nc.tensor.transpose(psY[q][:, j, :], Y[:, q, j * P:(j + 1) * P], ident[:])
                last.then_inc(s_psY, 1)

            def project(i, q):
                pe.wait_ge(s_YT, i + 1)
                if not isinstance(i, int) or i >= 2:
                    pe.wait_ge(s_O, i - 1)
                for j in range(KI):
                    last = nc.tensor.matmul(psO[q][:, 0:D], YT[:, q, j, :], WO[:, j, :], start=(j == 0), stop=(j == KI - 1))
                last.then_inc(s_psO, 1)

            turn(0, 0)
            turn(1, 1)
            project(0, 0)
            with pe.Fori(1, NT // 2) as p:
                turn(2 * p, 0)
                project(2 * p - 1, 1)
                turn(2 * p + 1, 1)
                project(2 * p, 0)
            project(NT - 1, 1)

        @block.scalar
        def _(act):
            def copy(i, q):
                act.wait_ge(s_psY, i + 1)
                if not isinstance(i, int) or i >= 2:
                    act.wait_ge(s_psO, i - 1)
                nc.scalar.activation(YT[:, q, :, ::-1], psY[q][:], ACT.Copy).then_inc(s_YT, 1)

            def stage(i, q):
                if not isinstance(i, int) or i >= 2:
                    act.wait_ge(s_psY, i - 1)
                nc.scalar.activation(Y[:, q, :], U[:, at(i), :].rearrange("p a d -> p (a d)"), ACT.Copy).then_inc(s_Y, 1)

            def store(i, q):
                act.wait_ge(s_O, i + 1)
                act.dma_start(out[bass.ts(i, P), :], O[:, q, :]).then_inc(s_out[q], 16)

            stage(0, 0)
            stage(1, 1)
            for q in range(NBUF):
                copy(q, q % 2)
                stage(q + 2, q % 2)
            with act.Fori(1, NT // NBUF - 1) as p:
                for q in range(NBUF):
                    copy(NBUF * p + q, q % 2)
                    stage(NBUF * p + q + 2, q % 2)
                    store(NBUF * p + q - NBUF, q)
            for q in range(NBUF):
                copy(NT - NBUF + q, q % 2)
                if q < 2:
                    stage(NT - NBUF + q + 2, q)
                store(NT - 2 * NBUF + q, q)
            for q in range(NBUF):
                store(NT - NBUF + q, q)
            for q in range(NBUF):
                act.wait_ge(s_out[q], 16 * (NT // NBUF))

        @block.vector
        def _(dve):
            def add(i, q, n):
                dve.wait_ge(s_psO, i + 1)
                dve.wait_ge(s_R[q], 16 * n + 16)
                if not isinstance(n, int):
                    dve.wait_ge(s_out[q], 16 * n)
                nc.vector.tensor_copy(gv[:, q % 2, :], TOPV[:, at(i), :].rearrange("p a k -> p (a k)")).then_inc(s_gv, 1)
                nc.vector.tensor_tensor(O[:, q, :], psO[q % 2][:, 0:D], R[:, q, :], ALU.add).then_inc(s_add, 1)
                dve.wait_ge(s_G[q], 32 * n + 32)
                dve.wait_ge(s_gv, i + 1)
                for k in range(TOPK):
                    dve.wait_ge(s_add, 2 * i + k + 1)
                    nc.vector.scalar_tensor_tensor(O[:, q, :], G[:, q, k, :], gv[:, q % 2, k:k + 1], O[:, q, :],
                                                   ALU.mult, ALU.add).then_inc(s_add if k == 0 else s_O, 1)
            for q in range(NBUF):
                add(q, q, 0)
            with dve.Fori(1, NT // NBUF) as p:
                for q in range(NBUF):
                    add(NBUF * p + q, q, p)


def program(nc, t, out):
    partial = nc.dram_tensor("partial", [NTOK, D], F32, kind="Internal")
    rows = nc.dram_tensor("rows", [(NE + 1) * REG, D], F32, kind="Internal")
    results = nc.dram_tensor("results", [NX * P, D], F32, kind="Internal")
    stash = nc.dram_tensor("stash", [NB, 3, P, GB, P], F32, kind="Internal")
    table = nc.dram_tensor("responses", [NG, TROWS, CG], F32, kind="Internal")
    with nc.sbuf_tensor("U", [P, NT, DIN], F32) as U:
        with (nc.sbuf_tensor("POS", [P, NT, TOPK], U32) as POS, nc.sbuf_tensor("TOPV", [P, NT, TOPK], F32) as TOPV,
              nc.sbuf_tensor("TAB", [1, 2, NX], I32) as TAB, nc.sbuf_tensor("IDX", [P, NT, TOPK], F32) as IDX,
              nc.sbuf_tensor("PF", [P, NT, TOPK], F32) as PF, nc.sbuf_tensor("shift", [P, NE], F32) as shift):
            route = POS, TOPV, TAB, IDX, PF, shift
            phase1(nc, t, U, route, partial, rows)
            powers_and_experts(nc, t, route, rows, results, table, stash)
            recurrence(nc, t, U, table, stash)
            phase3(nc, t, U, route, partial, results, out)


def kernel(L0_attn_x, L0_attn_norm_w, L0_attn_Win, L0_attn_b_in, L0_attn_conv_w, L0_attn_conv_b, L0_attn_A,
           L0_attn_Bm, L0_attn_Cm, L0_attn_Wout, L0_attn_b_out, L0_ffn_centroids, L0_ffn_expert_biases,
           L0_ffn_Wr, L0_ffn_br, L0_ffn_Ws, L0_ffn_bs):
    import concourse.bacc as bacc
    from concourse.bass_utils import run_bass_kernel_spmd

    def a(v):
        return np.asarray(v)

    def blocks(v, k):
        v = a(v)
        return v.reshape((k, P) + v.shape[1:]).swapaxes(0, 1)

    A = a(L0_attn_A)
    arrays = {
        "x": a(L0_attn_x).reshape(NTOK, D),
        "normw": blocks(L0_attn_norm_w, KD),
        "win": blocks(L0_attn_Win, KD),
        "b_in": blocks(L0_attn_b_in, KI),
        "conv_w": blocks(a(L0_attn_conv_w)[:, 0, :], KI),
        "conv_b": blocks(L0_attn_conv_b, KI),
        "A": A.reshape(NG, P, NST).transpose(1, 0, 2),
        "AT": A.transpose(0, 2, 1).reshape(NG, P, NST).transpose(1, 0, 2),
        "B": a(L0_attn_Bm).reshape(NG, P).T,
        "C": a(L0_attn_Cm).reshape(NG, P).T,
        "wout": blocks(L0_attn_Wout, KI),
        "b_out": a(L0_attn_b_out).reshape(1, D),
        "cT": blocks(a(L0_ffn_centroids).T, KD),
        "ebias": np.broadcast_to(a(L0_ffn_expert_biases)[None, :], (P, NE)),
        "wr": blocks(a(L0_ffn_Wr).transpose(2, 0, 1).reshape(D, NE * D), KD),
        "br": a(L0_ffn_br),
        "ws": blocks(a(L0_ffn_Ws).transpose(2, 0, 1), KD),
        "bs": a(L0_ffn_bs).reshape(1, NSH, D),
        "ident": np.eye(P, dtype=np.float32),
        "iota": np.tile(np.arange(NE, dtype=np.float32), (P, 1)),
        "before": np.triu(np.ones((P, P), np.float32), 1),
        "down": np.arange(P, dtype=np.float32)[:, None],
        "region": np.tile(np.arange(NE, dtype=np.float32) * REG, (P, 1)),
        "tileno": np.tile(np.arange(NX, dtype=np.float32), (NE, 1)),
        "keep": np.tile((np.arange(NT) % NCH != 0).astype(np.float32), (P, 1)),
        "own": (np.arange(P)[:, None] // NST == np.arange(CG)[None, :]).astype(np.float32),
    }
    nc = bacc.Bacc("TRN2", target_bir_lowering=False, num_devices=1)
    arrays = {f"in_{n}": np.ascontiguousarray(v) for n, v in arrays.items()}
    t = {n[3:]: nc.dram_tensor(n, v.shape, F32, kind="ExternalInput").ap() for n, v in arrays.items()}
    out = nc.dram_tensor("out_0", (NTOK, D), F32, kind="ExternalOutput").ap()
    program(nc, t, out)
    r = run_bass_kernel_spmd(nc, [arrays], core_ids=[0])
    return r.results[0]["out_0"].reshape(BATCH, SEQ, D)
```
